# Optimizing a Trainium2 kernel written in Bass

```python
import numpy as np
import jax
import jax.numpy as jnp

def _softmax(x, axis=-1):
    return jax.nn.softmax(x, axis=axis)

def _gelu(x):
    return jax.nn.gelu(x, approximate=True)

def _silu(x):
    return jax.nn.silu(x)

def _sigmoid(x):
    return jax.nn.sigmoid(x)

def _layernorm(x, axis=-1, eps=1e-05):
    m = jnp.mean(x, axis=axis, keepdims=True)
    v = jnp.var(x, axis=axis, keepdims=True)
    return (x - m) / jnp.sqrt(v + eps)

def _scatter_add(tgt, idx, src, axis=0):
    return tgt.at[idx].add(src)

def _segment_sum(src, seg, n):
    return jax.ops.segment_sum(src, seg, n)
kernel_name = 'mk_gps_d4_gnn_r32_71f0c4'

def setup_inputs(seed: int=0):
    np.random.seed(seed)
    _w = jnp.asarray

    def _rec_inputs():
        import jax
        import jax.numpy as jnp
        _gk = jax.random.key(seed)
        x = -6.415e-05 + 1 * jax.random.normal(jax.random.fold_in(_gk, 1), (625, 512), jnp.float32)
        src = jax.random.randint(jax.random.fold_in(_gk, 2), (10000,), 0, 625, jnp.int32)
        dst = jax.random.randint(jax.random.fold_in(_gk, 3), (10000,), 0, 625, jnp.int32)
        _o = jnp.argsort(dst, stable=True)
        src = src[_o]
        dst = dst[_o]
        edge_attr_8 = 0.0012443 + 1.0001 * jax.random.normal(jax.random.fold_in(_gk, 12), (10000, 8), jnp.float32)
        return (x, src, dst, edge_attr_8)
    x, src, dst, edge_attr_8 = _rec_inputs()

    def _L0_gnn_setup():
        import jax, jax.numpy as jnp
        import numpy as np
        N_NODES = 625
        N_EDGES = 10000
        D_IN = 512
        D_HID = 512
        EPS = 1e-05

        def _xavier(key, shape):
            fan_in, fan_out = (shape[1], shape[0])
            limit = np.sqrt(6.0 / (fan_in + fan_out)).astype(np.float32)
            return jax.random.uniform(key, shape, jnp.float32, -limit, limit)

        def _sage_conv(h, src, dst, Wl, bl, Wr):
            msg = h[src]
            s = jax.ops.segment_sum(msg, dst, num_segments=N_NODES)
            cnt = jax.ops.segment_sum(jnp.ones((src.shape[0], 1), h.dtype), dst, num_segments=N_NODES)
            agg = s / jnp.maximum(cnt, 1.0)
            return agg @ Wl.T + bl + h @ Wr.T

        def _layer_norm(h, g, b):
            mu = jnp.mean(h, axis=-1, keepdims=True)
            var = jnp.mean((h - mu) ** 2, axis=-1, keepdims=True)
            return (h - mu) * jax.lax.rsqrt(var + EPS) * g + b

        def _prelu(h, a):
            return jnp.where(h >= 0, h, a * h)
        key = jax.random.key(seed)
        ks = jax.random.split(key, 16)
        x = jax.random.normal(ks[0], (N_NODES, D_IN), jnp.float32)
        edge_index = jax.random.randint(ks[1], (2, N_EDGES), 0, N_NODES, jnp.int64)
        dims = [(D_IN, D_HID), (D_HID, D_HID), (D_HID, D_HID)]
        inp = {'x': x, 'edge_index': edge_index}
        for i, (din, dout) in enumerate(dims):
            inp[f'Wl{i}'] = _xavier(ks[2 + 3 * i], (dout, din))
            inp[f'bl{i}'] = jnp.zeros((dout,), jnp.float32)
            inp[f'Wr{i}'] = _xavier(ks[3 + 3 * i], (dout, din))
            inp[f'g{i}'] = jnp.ones((dout,), jnp.float32)
            inp[f'b{i}'] = jnp.zeros((dout,), jnp.float32)
        inp['a_prelu'] = jnp.full((1,), 0.25, jnp.float32)
        return inp
    _L0_gnn_all = _L0_gnn_setup()
    _L0_gnn_in = {k: v for k, v in _L0_gnn_all.items() if k in ('Wl0', 'bl0', 'Wr0', 'g0', 'b0', 'Wl1', 'bl1', 'Wr1', 'g1', 'b1', 'Wl2', 'bl2', 'Wr2', 'g2', 'b2', 'a_prelu')}
    del _L0_gnn_all

    def _L0_mix_setup():
        import jax, jax.numpy as jnp
        import numpy as np
        HEADS = 8
        DIM_HEAD = 64
        DIM = 512
        INNER = HEADS * DIM_HEAD
        SCALE = DIM_HEAD ** (-0.5)

        def _feature_map(t):
            return jax.nn.elu(t) + 1.0
        key = jax.random.key(seed)
        k1, k2, k3, k4 = jax.random.split(key, 4)
        b, n = (8, 128)
        x = jax.random.normal(k1, (b, n, DIM), dtype=jnp.float32)
        w_qkv = jax.random.normal(k2, (INNER * 3, DIM), dtype=jnp.float32) * DIM ** (-0.5)
        w_out = jax.random.normal(k3, (DIM, INNER), dtype=jnp.float32) * INNER ** (-0.5)
        b_out = jax.random.normal(k4, (DIM,), dtype=jnp.float32) * 0.01
        return {'x': x, 'w_qkv': w_qkv, 'w_out': w_out, 'b_out': b_out}
    _L0_mix_all = _L0_mix_setup()
    _L0_mix_in = {k: v for k, v in _L0_mix_all.items() if k in ('w_qkv', 'w_out', 'b_out')}
    del _L0_mix_all

    def _L0_ffn_setup():
        import jax, jax.numpy as jnp
        import numpy as np
        D_MODEL = 512
        DFF = 64
        TOP_K = 2
        EXPERTS_PER_LEVEL = (4, 8)

        def _moe_level(x, Wr, W1, b1, W2, b2, k):
            probs = jax.nn.softmax(jnp.einsum('bsd,de->bse', x, Wr), axis=-1)
            _, top_idx = jax.lax.top_k(probs, k)
            dispatch = jax.nn.one_hot(top_idx, probs.shape[-1], dtype=x.dtype).sum(axis=-2)
            xm = x[:, :, None, :] * dispatch[..., None]
            h = jax.nn.relu(jnp.einsum('bsed,edf->bsef', xm, W1) + b1)
            y = jnp.einsum('bsef,efd->bsed', h, W2) + b2
            return jnp.sum(y * probs[..., None], axis=2)
        key = jax.random.key(seed)
        ks = jax.random.split(key, 12)

        def w(k, fan_in, shape):
            return jax.random.normal(k, shape, jnp.float32) * (1.0 / np.sqrt(fan_in))

        def b(k, shape):
            return jax.random.normal(k, shape, jnp.float32) * 0.01
        E0, E1 = EXPERTS_PER_LEVEL
        return {'x': jax.random.normal(ks[0], (4, 64, D_MODEL), jnp.float32), 'Wr0': w(ks[1], D_MODEL, (D_MODEL, E0)), 'W1_0': w(ks[2], D_MODEL, (E0, D_MODEL, DFF)), 'b1_0': b(ks[3], (E0, DFF)), 'W2_0': w(ks[4], DFF, (E0, DFF, D_MODEL)), 'b2_0': b(ks[5], (E0, D_MODEL)), 'Wr1': w(ks[6], D_MODEL, (D_MODEL, E1)), 'W1_1': w(ks[7], D_MODEL, (E1, D_MODEL, DFF)), 'b1_1': b(ks[8], (E1, DFF)), 'W2_1': w(ks[9], DFF, (E1, DFF, D_MODEL)), 'b2_1': b(ks[10], (E1, D_MODEL))}
    _L0_ffn_all = _L0_ffn_setup()
    _L0_ffn_in = {k: v for k, v in _L0_ffn_all.items() if k in ('Wr0', 'W1_0', 'b1_0', 'W2_0', 'b2_0', 'Wr1', 'W1_1', 'b1_1', 'W2_1', 'b2_1')}
    del _L0_ffn_all

    def _L1_gnn_setup():
        import jax, jax.numpy as jnp
        import numpy as np
        N, E, D = (10000, 5000, 512)

        def _sage_layer(h, src, dst, W_self, W_neigh, b, n_nodes):
            agg = jax.ops.segment_sum(h[src], dst, num_segments=n_nodes)
            deg = jax.ops.segment_sum(jnp.ones_like(dst, dtype=h.dtype), dst, num_segments=n_nodes)
            h_neigh = agg / jnp.maximum(deg, 1.0)[:, None]
            return jax.nn.relu(h @ W_self + h_neigh @ W_neigh + b)
        key = jax.random.key(seed)
        ks = jax.random.split(key, 8)
        scale = 1.0 / np.sqrt(D)
        return {'feats': jax.random.normal(ks[0], (N, D), dtype=jnp.float32), 'src': jax.random.randint(ks[1], (E,), 0, N, dtype=jnp.int32), 'dst': jax.random.randint(ks[2], (E,), 0, N, dtype=jnp.int32), 'W_self1': jax.random.normal(ks[3], (D, D), dtype=jnp.float32) * scale, 'W_neigh1': jax.random.normal(ks[4], (D, D), dtype=jnp.float32) * scale, 'b1': jnp.zeros((D,), dtype=jnp.float32), 'W_self2': jax.random.normal(ks[5], (D, D), dtype=jnp.float32) * scale, 'W_neigh2': jax.random.normal(ks[6], (D, D), dtype=jnp.float32) * scale, 'b2': jnp.zeros((D,), dtype=jnp.float32)}
    _L1_gnn_all = _L1_gnn_setup()
    _L1_gnn_in = {k: v for k, v in _L1_gnn_all.items() if k in ('W_self1', 'W_neigh1', 'b1', 'W_self2', 'W_neigh2', 'b2')}
    del _L1_gnn_all

    def _L1_mix_setup():
        import jax, jax.numpy as jnp
        import numpy as np
        DIM = 512
        HEADS = 8
        DIM_HEAD = 64
        SLICE = 32
        INNER = HEADS * DIM_HEAD
        key = jax.random.key(seed)
        ks = jax.random.split(key, 8)
        B, N = (8, 256)
        s = 0.02
        return {'x': jax.random.normal(ks[0], (B, N, DIM), dtype=jnp.float32), 'W_in': jax.random.normal(ks[1], (DIM, INNER), dtype=jnp.float32) * s, 'b_in': jnp.zeros((INNER,), dtype=jnp.float32), 'Wq': jax.random.normal(ks[2], (DIM_HEAD, SLICE), dtype=jnp.float32) * s, 'Wk': jax.random.normal(ks[3], (DIM_HEAD, SLICE), dtype=jnp.float32) * s, 'Wv': jax.random.normal(ks[4], (DIM_HEAD, DIM_HEAD), dtype=jnp.float32) * s, 'W_out': jax.random.normal(ks[5], (INNER, DIM), dtype=jnp.float32) * s, 'b_out': jnp.zeros((DIM,), dtype=jnp.float32)}
    _L1_mix_all = _L1_mix_setup()
    _L1_mix_in = {k: v for k, v in _L1_mix_all.items() if k in ('W_in', 'b_in', 'Wq', 'Wk', 'Wv', 'W_out', 'b_out')}
    del _L1_mix_all

    def _L1_ffn_setup():
        import jax, jax.numpy as jnp
        import numpy as np
        INPUT_SIZE = 512
        HIDDEN_SIZE = 512
        key = jax.random.key(seed)
        ks = jax.random.split(key, 9)
        B, T, I, H = (64, 512, INPUT_SIZE, HIDDEN_SIZE)
        scale = 1.0 / np.sqrt(I + H)
        x = jax.random.normal(ks[0], (B, T, I), dtype=jnp.float32)

        def lin(kw, kb):
            W = jax.random.uniform(kw, (I + H, H), minval=-scale, maxval=scale, dtype=jnp.float32)
            b = jax.random.uniform(kb, (H,), minval=-scale, maxval=scale, dtype=jnp.float32)
            return (W, b)
        W_f, b_f = lin(ks[1], ks[2])
        W_i, b_i = lin(ks[3], ks[4])
        W_c, b_c = lin(ks[5], ks[6])
        W_o, b_o = lin(ks[7], ks[8])
        return {'x': x, 'W_f': W_f, 'b_f': b_f, 'W_i': W_i, 'b_i': b_i, 'W_c': W_c, 'b_c': b_c, 'W_o': W_o, 'b_o': b_o}
    _L1_ffn_all = _L1_ffn_setup()
    _L1_ffn_in = {k: v for k, v in _L1_ffn_all.items() if k in ('W_f', 'b_f', 'W_i', 'b_i', 'W_c', 'b_c', 'W_o', 'b_o')}
    del _L1_ffn_all

    def _L2_gnn_setup():
        import jax, jax.numpy as jnp
        import numpy as np
        N = 625
        E = 10000
        D = 512
        H = 8
        DK = D // H
        key = jax.random.key(seed)
        ks = jax.random.split(key, 12)
        x = jax.random.normal(ks[0], (N, D), jnp.float32)
        rows = jnp.sort(jax.random.randint(ks[1], (E,), 0, N))
        cols = jax.random.randint(ks[2], (E,), 0, N)
        edge_index = jnp.stack([rows, cols]).astype(jnp.int32)
        att_bias = jax.random.normal(ks[3], (E, H), jnp.float32)
        s = float(1.0 / np.sqrt(D))
        Wq = jax.random.normal(ks[4], (D, D), jnp.float32) * s
        Wk = jax.random.normal(ks[5], (D, D), jnp.float32) * s
        Wv = jax.random.normal(ks[6], (D, D), jnp.float32) * s
        Wo = jax.random.normal(ks[7], (D, D), jnp.float32) * s
        bq = jnp.zeros((D,), jnp.float32)
        bk = jnp.zeros((D,), jnp.float32)
        bv = jnp.zeros((D,), jnp.float32)
        bo = jnp.zeros((D,), jnp.float32)
        return dict(x=x, edge_index=edge_index, att_bias=att_bias, Wq=Wq, bq=bq, Wk=Wk, bk=bk, Wv=Wv, bv=bv, Wo=Wo, bo=bo)
    _L2_gnn_all = _L2_gnn_setup()
    _L2_gnn_in = {k: v for k, v in _L2_gnn_all.items() if k in ('Wq', 'bq', 'Wk', 'bk', 'Wv', 'bv', 'Wo', 'bo')}
    del _L2_gnn_all

    def _L2_mix_setup():
        import jax, jax.numpy as jnp
        import numpy as np
        B, N, C = (8, 256, 512)
        H = 8
        D = C // H
        EPS = 1e-06

        def _linear_attention(q, k, v):
            qf = jax.nn.elu(q) + 1.0
            kf = jax.nn.elu(k) + 1.0
            kv = jnp.einsum('bhnd,bhne->bhde', kf, v)
            z = jnp.einsum('bhnd,bhd->bhn', qf, kf.sum(axis=2))
            out = jnp.einsum('bhnd,bhde->bhne', qf, kv) / (z[..., None] + EPS)
            return out
        key = jax.random.key(seed)
        k1, k2, k3, k4 = jax.random.split(key, 4)
        x = jax.random.normal(k1, (B, N, C), dtype=jnp.float32)
        w_qkv = jax.random.normal(k2, (C, 3 * C), dtype=jnp.float32) * (1.0 / np.sqrt(C))
        w_proj = jax.random.normal(k3, (C, C), dtype=jnp.float32) * (1.0 / np.sqrt(C))
        b_proj = jax.random.normal(k4, (C,), dtype=jnp.float32) * 0.01
        return {'x': x, 'w_qkv': w_qkv, 'w_proj': w_proj, 'b_proj': b_proj}
    _L2_mix_all = _L2_mix_setup()
    _L2_mix_in = {k: v for k, v in _L2_mix_all.items() if k in ('w_qkv', 'w_proj', 'b_proj')}
    del _L2_mix_all

    def _L2_ffn_setup():
        import jax, jax.numpy as jnp
        import numpy as np
        B, S, H, E, K, DF, SH = (8, 128, 512, 8, 2, 128, 512)
        key = jax.random.key(seed)
        ks = jax.random.split(key, 10)
        n = lambda i, shape, sc: jax.random.normal(ks[i], shape, jnp.float32) * sc
        return {'hidden_states': n(0, (B, S, H), 1.0), 'gate_w': n(1, (E, H), 0.05), 'w1': n(2, (E, H, DF), 0.05), 'b1': n(3, (E, DF), 0.01), 'w2': n(4, (E, DF, H), 0.05), 'b2': n(5, (E, H), 0.01), 'sw1': n(6, (H, SH), 0.05), 'sb1': n(7, (SH,), 0.01), 'sw2': n(8, (SH, H), 0.05), 'sb2': n(9, (H,), 0.01)}
    _L2_ffn_all = _L2_ffn_setup()
    _L2_ffn_in = {k: v for k, v in _L2_ffn_all.items() if k in ('gate_w', 'w1', 'b1', 'w2', 'b2', 'sw1', 'sb1', 'sw2', 'sb2')}
    del _L2_ffn_all

    def _L3_gnn_setup():
        import jax, jax.numpy as jnp
        import numpy as np
        N, E = (625, 20000)
        LATENT, HID, OUT, HEADS = (512, 256, 128, 2)
        NEG_SLOPE = 0.2

        def _gat_conv(x, edge_index, Wg, att_src, att_dst, bias_g):
            n = x.shape[0]
            loops = jnp.tile(jnp.arange(n, dtype=edge_index.dtype)[None, :], (2, 1))
            ei = jnp.concatenate([edge_index, loops], axis=1)
            src, dst = (ei[0], ei[1])
            xp = (x @ Wg).reshape(n, HEADS, OUT)
            a_src = jnp.einsum('nhc,hc->nh', xp, att_src)
            a_dst = jnp.einsum('nhc,hc->nh', xp, att_dst)
            alpha = jax.nn.leaky_relu(a_src[src] + a_dst[dst], NEG_SLOPE)
            amax = jax.ops.segment_max(alpha, dst, num_segments=n)
            alpha = jnp.exp(alpha - amax[dst])
            denom = jax.ops.segment_sum(alpha, dst, num_segments=n)
            alpha = alpha / jnp.maximum(denom[dst], 1e-16)
            msg = xp[src] * alpha[:, :, None]
            out = jax.ops.segment_sum(msg, dst, num_segments=n)
            return out.reshape(n, HEADS * OUT) + bias_g
        key = jax.random.key(seed)
        ks = jax.random.split(key, 12)
        s = 0.02
        return {'z': jax.random.normal(ks[0], (N, LATENT), dtype=jnp.float32), 'edge_index': jax.random.randint(ks[1], (2, E), 0, N, dtype=jnp.int64), 'W1': jax.random.normal(ks[2], (LATENT, HID), dtype=jnp.float32) * s, 'b1': jnp.zeros((HID,), dtype=jnp.float32), 'W2': jax.random.normal(ks[3], (HID, HID * HEADS), dtype=jnp.float32) * s, 'b2': jnp.zeros((HID * HEADS,), dtype=jnp.float32), 'Wg': jax.random.normal(ks[4], (HID * HEADS, HEADS * OUT), dtype=jnp.float32) * s, 'att_src': jax.random.normal(ks[5], (HEADS, OUT), dtype=jnp.float32) * s, 'att_dst': jax.random.normal(ks[6], (HEADS, OUT), dtype=jnp.float32) * s, 'bias_g': jnp.zeros((HEADS * OUT,), dtype=jnp.float32), 'W3': jax.random.normal(ks[7], (OUT * HEADS, 512), dtype=jnp.float32) * s, 'b3': jnp.zeros((512,), dtype=jnp.float32)}
    _L3_gnn_all = _L3_gnn_setup()
    _L3_gnn_in = {k: v for k, v in _L3_gnn_all.items() if k in ('W1', 'b1', 'W2', 'b2', 'Wg', 'att_src', 'att_dst', 'bias_g', 'W3', 'b3')}
    del _L3_gnn_all

    def _L3_mix_setup():
        import jax, jax.numpy as jnp
        import numpy as np
        D_MODEL = 512
        NUM_HEADS = 8
        HEAD_DIM = D_MODEL // NUM_HEADS
        LN_EPS = 1e-05

        def _split_heads(t, B, S):
            return t.reshape(B, S, NUM_HEADS, HEAD_DIM).transpose(0, 2, 1, 3)

        def _feature_map(t):
            return jax.nn.elu(t) + 1.0
        key = jax.random.key(seed)
        ks = jax.random.split(key, 12)
        B, S, D = (4, 256, D_MODEL)
        scale = 1.0 / np.sqrt(D)
        inp = {'x': jax.random.normal(ks[0], (B, S, D), dtype=jnp.float32), 'Wq': jax.random.normal(ks[1], (D, D), dtype=jnp.float32) * scale, 'bq': jnp.zeros((D,), dtype=jnp.float32), 'Wk': jax.random.normal(ks[2], (D, D), dtype=jnp.float32) * scale, 'bk': jnp.zeros((D,), dtype=jnp.float32), 'Wv': jax.random.normal(ks[3], (D, D), dtype=jnp.float32) * scale, 'bv': jnp.zeros((D,), dtype=jnp.float32), 'Wo': jax.random.normal(ks[4], (D, D), dtype=jnp.float32) * scale, 'bo': jnp.zeros((D,), dtype=jnp.float32), 'gamma': jnp.ones((D,), dtype=jnp.float32), 'beta': jnp.zeros((D,), dtype=jnp.float32)}
        return inp
    _L3_mix_all = _L3_mix_setup()
    _L3_mix_in = {k: v for k, v in _L3_mix_all.items() if k in ('Wq', 'bq', 'Wk', 'bk', 'Wv', 'bv', 'Wo', 'bo', 'gamma', 'beta')}
    del _L3_mix_all

    def _L3_ffn_setup():
        import jax, jax.numpy as jnp
        import numpy as np
        S, B, I, O, H, E, K = (128, 32, 512, 512, 512, 8, 2)

        def _expert(x_seq, Wi, Wh, b, Wo, bo):
            Bsz = x_seq.shape[1]
            Hd = Wh.shape[0]

            def step(carry, xt):
                h, c = carry
                gates = xt @ Wi + h @ Wh + b
                i_, f_, g_, o_ = jnp.split(gates, 4, axis=-1)
                c = jax.nn.sigmoid(f_) * c + jax.nn.sigmoid(i_) * jnp.tanh(g_)
                h = jax.nn.sigmoid(o_) * jnp.tanh(c)
                return ((h, c), h @ Wo + bo)
            init = (jnp.zeros((Bsz, Hd), x_seq.dtype), jnp.zeros((Bsz, Hd), x_seq.dtype))
            _, ys = jax.lax.scan(step, init, x_seq)
            return ys
        key = jax.random.key(seed)
        ks = jax.random.split(key, 6)
        s = 0.02
        return {'x': jax.random.normal(ks[0], (S, B, I), dtype=jnp.float32), 'router_w': jax.random.normal(ks[1], (I, E), dtype=jnp.float32) * s, 'router_b': jnp.zeros((E,), dtype=jnp.float32), 'Wi': jax.random.normal(ks[2], (E, I, 4 * H), dtype=jnp.float32) * s, 'Wh': jax.random.normal(ks[3], (E, H, 4 * H), dtype=jnp.float32) * s, 'b': jnp.zeros((E, 4 * H), dtype=jnp.float32), 'Wo': jax.random.normal(ks[4], (E, H, O), dtype=jnp.float32) * s, 'bo': jnp.zeros((E, O), dtype=jnp.float32)}
    _L3_ffn_all = _L3_ffn_setup()
    _L3_ffn_in = {k: v for k, v in _L3_ffn_all.items() if k in ('router_w', 'router_b', 'Wi', 'Wh', 'b', 'Wo', 'bo')}
    del _L3_ffn_all
    return {'x': x, 'src': src, 'dst': dst, 'edge_attr_8': edge_attr_8, 'L0_gnn_Wl0': _L0_gnn_in['Wl0'], 'L0_gnn_bl0': _L0_gnn_in['bl0'], 'L0_gnn_Wr0': _L0_gnn_in['Wr0'], 'L0_gnn_g0': _L0_gnn_in['g0'], 'L0_gnn_b0': _L0_gnn_in['b0'], 'L0_gnn_Wl1': _L0_gnn_in['Wl1'], 'L0_gnn_bl1': _L0_gnn_in['bl1'], 'L0_gnn_Wr1': _L0_gnn_in['Wr1'], 'L0_gnn_g1': _L0_gnn_in['g1'], 'L0_gnn_b1': _L0_gnn_in['b1'], 'L0_gnn_Wl2': _L0_gnn_in['Wl2'], 'L0_gnn_bl2': _L0_gnn_in['bl2'], 'L0_gnn_Wr2': _L0_gnn_in['Wr2'], 'L0_gnn_g2': _L0_gnn_in['g2'], 'L0_gnn_b2': _L0_gnn_in['b2'], 'L0_gnn_a_prelu': _L0_gnn_in['a_prelu'], 'L0_mix_w_qkv': _L0_mix_in['w_qkv'], 'L0_mix_w_out': _L0_mix_in['w_out'], 'L0_mix_b_out': _L0_mix_in['b_out'], 'L0_ffn_Wr0': _L0_ffn_in['Wr0'], 'L0_ffn_W1_0': _L0_ffn_in['W1_0'], 'L0_ffn_b1_0': _L0_ffn_in['b1_0'], 'L0_ffn_W2_0': _L0_ffn_in['W2_0'], 'L0_ffn_b2_0': _L0_ffn_in['b2_0'], 'L0_ffn_Wr1': _L0_ffn_in['Wr1'], 'L0_ffn_W1_1': _L0_ffn_in['W1_1'], 'L0_ffn_b1_1': _L0_ffn_in['b1_1'], 'L0_ffn_W2_1': _L0_ffn_in['W2_1'], 'L0_ffn_b2_1': _L0_ffn_in['b2_1'], 'L1_gnn_W_self1': _L1_gnn_in['W_self1'], 'L1_gnn_W_neigh1': _L1_gnn_in['W_neigh1'], 'L1_gnn_b1': _L1_gnn_in['b1'], 'L1_gnn_W_self2': _L1_gnn_in['W_self2'], 'L1_gnn_W_neigh2': _L1_gnn_in['W_neigh2'], 'L1_gnn_b2': _L1_gnn_in['b2'], 'L1_mix_W_in': _L1_mix_in['W_in'], 'L1_mix_b_in': _L1_mix_in['b_in'], 'L1_mix_Wq': _L1_mix_in['Wq'], 'L1_mix_Wk': _L1_mix_in['Wk'], 'L1_mix_Wv': _L1_mix_in['Wv'], 'L1_mix_W_out': _L1_mix_in['W_out'], 'L1_mix_b_out': _L1_mix_in['b_out'], 'L1_ffn_W_f': _L1_ffn_in['W_f'], 'L1_ffn_b_f': _L1_ffn_in['b_f'], 'L1_ffn_W_i': _L1_ffn_in['W_i'], 'L1_ffn_b_i': _L1_ffn_in['b_i'], 'L1_ffn_W_c': _L1_ffn_in['W_c'], 'L1_ffn_b_c': _L1_ffn_in['b_c'], 'L1_ffn_W_o': _L1_ffn_in['W_o'], 'L1_ffn_b_o': _L1_ffn_in['b_o'], 'L2_gnn_Wq': _L2_gnn_in['Wq'], 'L2_gnn_bq': _L2_gnn_in['bq'], 'L2_gnn_Wk': _L2_gnn_in['Wk'], 'L2_gnn_bk': _L2_gnn_in['bk'], 'L2_gnn_Wv': _L2_gnn_in['Wv'], 'L2_gnn_bv': _L2_gnn_in['bv'], 'L2_gnn_Wo': _L2_gnn_in['Wo'], 'L2_gnn_bo': _L2_gnn_in['bo'], 'L2_mix_w_qkv': _L2_mix_in['w_qkv'], 'L2_mix_w_proj': _L2_mix_in['w_proj'], 'L2_mix_b_proj': _L2_mix_in['b_proj'], 'L2_ffn_gate_w': _L2_ffn_in['gate_w'], 'L2_ffn_w1': _L2_ffn_in['w1'], 'L2_ffn_b1': _L2_ffn_in['b1'], 'L2_ffn_w2': _L2_ffn_in['w2'], 'L2_ffn_b2': _L2_ffn_in['b2'], 'L2_ffn_sw1': _L2_ffn_in['sw1'], 'L2_ffn_sb1': _L2_ffn_in['sb1'], 'L2_ffn_sw2': _L2_ffn_in['sw2'], 'L2_ffn_sb2': _L2_ffn_in['sb2'], 'L3_gnn_W1': _L3_gnn_in['W1'], 'L3_gnn_b1': _L3_gnn_in['b1'], 'L3_gnn_W2': _L3_gnn_in['W2'], 'L3_gnn_b2': _L3_gnn_in['b2'], 'L3_gnn_Wg': _L3_gnn_in['Wg'], 'L3_gnn_att_src': _L3_gnn_in['att_src'], 'L3_gnn_att_dst': _L3_gnn_in['att_dst'], 'L3_gnn_bias_g': _L3_gnn_in['bias_g'], 'L3_gnn_W3': _L3_gnn_in['W3'], 'L3_gnn_b3': _L3_gnn_in['b3'], 'L3_mix_Wq': _L3_mix_in['Wq'], 'L3_mix_bq': _L3_mix_in['bq'], 'L3_mix_Wk': _L3_mix_in['Wk'], 'L3_mix_bk': _L3_mix_in['bk'], 'L3_mix_Wv': _L3_mix_in['Wv'], 'L3_mix_bv': _L3_mix_in['bv'], 'L3_mix_Wo': _L3_mix_in['Wo'], 'L3_mix_bo': _L3_mix_in['bo'], 'L3_mix_gamma': _L3_mix_in['gamma'], 'L3_mix_beta': _L3_mix_in['beta'], 'L3_ffn_router_w': _L3_ffn_in['router_w'], 'L3_ffn_router_b': _L3_ffn_in['router_b'], 'L3_ffn_Wi': _L3_ffn_in['Wi'], 'L3_ffn_Wh': _L3_ffn_in['Wh'], 'L3_ffn_b': _L3_ffn_in['b'], 'L3_ffn_Wo': _L3_ffn_in['Wo'], 'L3_ffn_bo': _L3_ffn_in['bo']}

def reference(x, src, dst, edge_attr_8, L0_gnn_Wl0, L0_gnn_bl0, L0_gnn_Wr0, L0_gnn_g0, L0_gnn_b0, L0_gnn_Wl1, L0_gnn_bl1, L0_gnn_Wr1, L0_gnn_g1, L0_gnn_b1, L0_gnn_Wl2, L0_gnn_bl2, L0_gnn_Wr2, L0_gnn_g2, L0_gnn_b2, L0_gnn_a_prelu, L0_mix_w_qkv, L0_mix_w_out, L0_mix_b_out, L0_ffn_Wr0, L0_ffn_W1_0, L0_ffn_b1_0, L0_ffn_W2_0, L0_ffn_b2_0, L0_ffn_Wr1, L0_ffn_W1_1, L0_ffn_b1_1, L0_ffn_W2_1, L0_ffn_b2_1, L1_gnn_W_self1, L1_gnn_W_neigh1, L1_gnn_b1, L1_gnn_W_self2, L1_gnn_W_neigh2, L1_gnn_b2, L1_mix_W_in, L1_mix_b_in, L1_mix_Wq, L1_mix_Wk, L1_mix_Wv, L1_mix_W_out, L1_mix_b_out, L1_ffn_W_f, L1_ffn_b_f, L1_ffn_W_i, L1_ffn_b_i, L1_ffn_W_c, L1_ffn_b_c, L1_ffn_W_o, L1_ffn_b_o, L2_gnn_Wq, L2_gnn_bq, L2_gnn_Wk, L2_gnn_bk, L2_gnn_Wv, L2_gnn_bv, L2_gnn_Wo, L2_gnn_bo, L2_mix_w_qkv, L2_mix_w_proj, L2_mix_b_proj, L2_ffn_gate_w, L2_ffn_w1, L2_ffn_b1, L2_ffn_w2, L2_ffn_b2, L2_ffn_sw1, L2_ffn_sb1, L2_ffn_sw2, L2_ffn_sb2, L3_gnn_W1, L3_gnn_b1, L3_gnn_W2, L3_gnn_b2, L3_gnn_Wg, L3_gnn_att_src, L3_gnn_att_dst, L3_gnn_bias_g, L3_gnn_W3, L3_gnn_b3, L3_mix_Wq, L3_mix_bq, L3_mix_Wk, L3_mix_bk, L3_mix_Wv, L3_mix_bv, L3_mix_Wo, L3_mix_bo, L3_mix_gamma, L3_mix_beta, L3_ffn_router_w, L3_ffn_router_b, L3_ffn_Wi, L3_ffn_Wh, L3_ffn_b, L3_ffn_Wo, L3_ffn_bo):
    import jax
    import jax.numpy as jnp

    def _L0_gnn_ref(x, edge_index, Wl0, bl0, Wr0, g0, b0, Wl1, bl1, Wr1, g1, b1, Wl2, bl2, Wr2, g2, b2, a_prelu):
        import jax, jax.numpy as jnp
        import numpy as np
        N_NODES = 625
        N_EDGES = 10000
        D_IN = 512
        D_HID = 512
        EPS = 1e-05

        def _xavier(key, shape):
            fan_in, fan_out = (shape[1], shape[0])
            limit = np.sqrt(6.0 / (fan_in + fan_out)).astype(np.float32)
            return jax.random.uniform(key, shape, jnp.float32, -limit, limit)

        def _sage_conv(h, src, dst, Wl, bl, Wr):
            msg = h[src]
            s = jax.ops.segment_sum(msg, dst, num_segments=N_NODES)
            cnt = jax.ops.segment_sum(jnp.ones((src.shape[0], 1), h.dtype), dst, num_segments=N_NODES)
            agg = s / jnp.maximum(cnt, 1.0)
            return agg @ Wl.T + bl + h @ Wr.T

        def _layer_norm(h, g, b):
            mu = jnp.mean(h, axis=-1, keepdims=True)
            var = jnp.mean((h - mu) ** 2, axis=-1, keepdims=True)
            return (h - mu) * jax.lax.rsqrt(var + EPS) * g + b

        def _prelu(h, a):
            return jnp.where(h >= 0, h, a * h)
        src, dst = (edge_index[0], edge_index[1])
        params = [(Wl0, bl0, Wr0, g0, b0), (Wl1, bl1, Wr1, g1, b1), (Wl2, bl2, Wr2, g2, b2)]
        h = x
        residual = 0.0
        for Wl, bl, Wr, g, b in params:
            h = residual + _sage_conv(h, src, dst, Wl, bl, Wr)
            h = _layer_norm(h, g, b)
            h = _prelu(h, a_prelu)
            residual = h
        return h

    def _L0_mix_ref(x, w_qkv, w_out, b_out):
        import jax, jax.numpy as jnp
        import numpy as np
        HEADS = 8
        DIM_HEAD = 64
        DIM = 512
        INNER = HEADS * DIM_HEAD
        SCALE = DIM_HEAD ** (-0.5)

        def _feature_map(t):
            return jax.nn.elu(t) + 1.0
        b, n, _ = x.shape
        h, d = (HEADS, DIM_HEAD)
        qkv = x @ w_qkv.T
        q, k, v = jnp.split(qkv, 3, axis=-1)
        reshape = lambda t: t.reshape(b, n, h, d).transpose(0, 2, 1, 3)
        q, k, v = (reshape(q), reshape(k), reshape(v))
        q = _feature_map(q * SCALE)
        k = _feature_map(k)
        k_cumsum = k.sum(axis=2)
        context = jnp.einsum('bhnd,bhne->bhde', k, v)
        out = jnp.einsum('bhnd,bhde->bhne', q, context)
        denom = jnp.einsum('bhnd,bhd->bhn', q, k_cumsum)[..., None] + 1e-08
        out = out / denom
        out = out.transpose(0, 2, 1, 3).reshape(b, n, h * d)
        return out @ w_out.T + b_out

    def _L0_ffn_ref(x, Wr0, W1_0, b1_0, W2_0, b2_0, Wr1, W1_1, b1_1, W2_1, b2_1):
        import jax, jax.numpy as jnp
        import numpy as np
        D_MODEL = 512
        DFF = 64
        TOP_K = 2
        EXPERTS_PER_LEVEL = (4, 8)

        def _moe_level(x, Wr, W1, b1, W2, b2, k):
            probs = jax.nn.softmax(jnp.einsum('bsd,de->bse', x, Wr), axis=-1)
            _, top_idx = jax.lax.top_k(probs, k)
            dispatch = jax.nn.one_hot(top_idx, probs.shape[-1], dtype=x.dtype).sum(axis=-2)
            xm = x[:, :, None, :] * dispatch[..., None]
            h = jax.nn.relu(jnp.einsum('bsed,edf->bsef', xm, W1) + b1)
            y = jnp.einsum('bsef,efd->bsed', h, W2) + b2
            return jnp.sum(y * probs[..., None], axis=2)
        h0 = _moe_level(x, Wr0, W1_0, b1_0, W2_0, b2_0, TOP_K)
        out = _moe_level(h0, Wr1, W1_1, b1_1, W2_1, b2_1, TOP_K)
        return out

    def _L1_gnn_ref(feats, src, dst, W_self1, W_neigh1, b1, W_self2, W_neigh2, b2):
        import jax, jax.numpy as jnp
        import numpy as np
        N, E, D = (10000, 5000, 512)

        def _sage_layer(h, src, dst, W_self, W_neigh, b, n_nodes):
            agg = jax.ops.segment_sum(h[src], dst, num_segments=n_nodes)
            deg = jax.ops.segment_sum(jnp.ones_like(dst, dtype=h.dtype), dst, num_segments=n_nodes)
            h_neigh = agg / jnp.maximum(deg, 1.0)[:, None]
            return jax.nn.relu(h @ W_self + h_neigh @ W_neigh + b)
        n_nodes = feats.shape[0]
        h = _sage_layer(feats, src, dst, W_self1, W_neigh1, b1, n_nodes)
        h = _sage_layer(h, src, dst, W_self2, W_neigh2, b2, n_nodes)
        return h

    def _L1_mix_ref(x, W_in, b_in, Wq, Wk, Wv, W_out, b_out):
        import jax, jax.numpy as jnp
        import numpy as np
        DIM = 512
        HEADS = 8
        DIM_HEAD = 64
        SLICE = 32
        INNER = HEADS * DIM_HEAD
        B, N, C = x.shape
        x_mid = (x @ W_in + b_in).reshape(B, N, HEADS, DIM_HEAD).transpose(0, 2, 1, 3)
        q = x_mid @ Wq
        k = x_mid @ Wk
        v = x_mid @ Wv
        q = jax.nn.softmax(q, axis=-1)
        k = jax.nn.softmax(k, axis=-2)
        kv = jnp.einsum('bhns,bhnc->bhsc', k, v)
        qkv = jnp.einsum('bhns,bhsc->bhnc', q, kv)
        qkv = qkv.transpose(0, 2, 1, 3).reshape(B, N, INNER)
        return qkv @ W_out + b_out

    def _L1_ffn_ref(x, W_f, b_f, W_i, b_i, W_c, b_c, W_o, b_o):
        import jax, jax.numpy as jnp
        import numpy as np
        INPUT_SIZE = 512
        HIDDEN_SIZE = 512
        B, T, I = x.shape
        H = W_f.shape[1]
        h0 = jnp.zeros((B, H), dtype=x.dtype)
        c0 = jnp.zeros((B, H), dtype=x.dtype)

        def step(carry, x_t):
            h_prev, c_prev = carry
            combined = jnp.concatenate((x_t, h_prev), axis=1)
            f_t = jax.nn.sigmoid(combined @ W_f + b_f)
            i_t = jax.nn.sigmoid(combined @ W_i + b_i)
            c_tilde = jnp.tanh(combined @ W_c + b_c)
            c_t = f_t * c_prev + i_t * c_tilde
            o_t = jax.nn.sigmoid(combined @ W_o + b_o)
            h_t = o_t * jnp.tanh(c_t)
            return ((h_t, c_t), h_t)
        _, hs = jax.lax.scan(step, (h0, c0), jnp.swapaxes(x, 0, 1))
        return jnp.swapaxes(hs, 0, 1)

    def _L2_gnn_ref(x, edge_index, att_bias, Wq, bq, Wk, bk, Wv, bv, Wo, bo):
        import jax, jax.numpy as jnp
        import numpy as np
        N = 625
        E = 10000
        D = 512
        H = 8
        DK = D // H
        n = x.shape[0]
        rows, cols = (edge_index[0], edge_index[1])
        q = (x @ Wq + bq).reshape(n, H, DK)
        k = (x @ Wk + bk).reshape(n, H, DK)
        v = (x @ Wv + bv).reshape(n, H, DK)
        scale = 1.0 / jnp.sqrt(jnp.asarray(DK, x.dtype))
        logits = jnp.einsum('ehd,ehd->eh', q[rows] * scale, k[cols]) + att_bias
        row_max = jax.ops.segment_max(logits, rows, num_segments=n)
        p = jnp.exp(logits - row_max[rows])
        denom = jax.ops.segment_sum(p, rows, num_segments=n)
        att = p / denom[rows]
        y = jax.ops.segment_sum(att[:, :, None] * v[cols], rows, num_segments=n)
        out = y.reshape(n, H * DK) @ Wo + bo
        return out

    def _L2_mix_ref(x, w_qkv, w_proj, b_proj):
        import jax, jax.numpy as jnp
        import numpy as np
        B, N, C = (8, 256, 512)
        H = 8
        D = C // H
        EPS = 1e-06

        def _linear_attention(q, k, v):
            qf = jax.nn.elu(q) + 1.0
            kf = jax.nn.elu(k) + 1.0
            kv = jnp.einsum('bhnd,bhne->bhde', kf, v)
            z = jnp.einsum('bhnd,bhd->bhn', qf, kf.sum(axis=2))
            out = jnp.einsum('bhnd,bhde->bhne', qf, kv) / (z[..., None] + EPS)
            return out
        b, n, c = x.shape
        qkv = x @ w_qkv
        qkv = qkv.reshape(b, n, 3, H, D).transpose(2, 0, 3, 1, 4)
        q, k, v = (qkv[0], qkv[1], qkv[2])
        attn = _linear_attention(q, k, v)
        y = attn.transpose(0, 2, 1, 3).reshape(b, n, c)
        return y @ w_proj + b_proj

    def _L2_ffn_ref(hidden_states, gate_w, w1, b1, w2, b2, sw1, sb1, sw2, sb2):
        import jax, jax.numpy as jnp
        import numpy as np
        B, S, H, E, K, DF, SH = (8, 128, 512, 8, 2, 128, 512)
        x = hidden_states
        xf = x.reshape(-1, x.shape[-1])
        T = xf.shape[0]
        scores = jax.nn.softmax(xf @ gate_w.T, axis=-1)
        topk_w, topk_i = jax.lax.top_k(scores, K)
        topk_w = topk_w / (topk_w.sum(-1, keepdims=True) + 1e-20)
        combine = jnp.zeros((T, E), xf.dtype).at[jnp.arange(T)[:, None], topk_i].add(topk_w)
        h1 = jax.nn.relu(jnp.einsum('th,ehf->tef', xf, w1) + b1)
        eo = jnp.einsum('tef,efh->teh', h1, w2) + b2
        y = jnp.einsum('te,teh->th', combine, eo)
        shared = jax.nn.relu(xf @ sw1 + sb1) @ sw2 + sb2
        return (y + shared).reshape(x.shape)

    def _L3_gnn_ref(z, edge_index, W1, b1, W2, b2, Wg, att_src, att_dst, bias_g, W3, b3):
        import jax, jax.numpy as jnp
        import numpy as np
        N, E = (625, 20000)
        LATENT, HID, OUT, HEADS = (512, 256, 128, 2)
        NEG_SLOPE = 0.2

        def _gat_conv(x, edge_index, Wg, att_src, att_dst, bias_g):
            n = x.shape[0]
            loops = jnp.tile(jnp.arange(n, dtype=edge_index.dtype)[None, :], (2, 1))
            ei = jnp.concatenate([edge_index, loops], axis=1)
            src, dst = (ei[0], ei[1])
            xp = (x @ Wg).reshape(n, HEADS, OUT)
            a_src = jnp.einsum('nhc,hc->nh', xp, att_src)
            a_dst = jnp.einsum('nhc,hc->nh', xp, att_dst)
            alpha = jax.nn.leaky_relu(a_src[src] + a_dst[dst], NEG_SLOPE)
            amax = jax.ops.segment_max(alpha, dst, num_segments=n)
            alpha = jnp.exp(alpha - amax[dst])
            denom = jax.ops.segment_sum(alpha, dst, num_segments=n)
            alpha = alpha / jnp.maximum(denom[dst], 1e-16)
            msg = xp[src] * alpha[:, :, None]
            out = jax.ops.segment_sum(msg, dst, num_segments=n)
            return out.reshape(n, HEADS * OUT) + bias_g
        x = jax.nn.relu(z @ W1 + b1)
        x = jax.nn.relu(x @ W2 + b2)
        x = _gat_conv(x, edge_index, Wg, att_src, att_dst, bias_g)
        return x @ W3 + b3

    def _L3_mix_ref(x, Wq, bq, Wk, bk, Wv, bv, Wo, bo, gamma, beta):
        import jax, jax.numpy as jnp
        import numpy as np
        D_MODEL = 512
        NUM_HEADS = 8
        HEAD_DIM = D_MODEL // NUM_HEADS
        LN_EPS = 1e-05

        def _split_heads(t, B, S):
            return t.reshape(B, S, NUM_HEADS, HEAD_DIM).transpose(0, 2, 1, 3)

        def _feature_map(t):
            return jax.nn.elu(t) + 1.0
        B, S, D = x.shape
        q = _split_heads(x @ Wq + bq, B, S)
        k = _split_heads(x @ Wk + bk, B, S)
        v = _split_heads(x @ Wv + bv, B, S)
        q = _feature_map(q)
        k = _feature_map(k)
        kv = jnp.einsum('bhnd,bhnm->bhdm', k, v)
        out = jnp.einsum('bhnd,bhdm->bhnm', q, kv)
        k_sum = k.sum(axis=2)
        normalizer = jnp.clip(jnp.einsum('bhnd,bhd->bhn', q, k_sum), 1e-06, None)
        out = out / normalizer[..., None]
        out = out.transpose(0, 2, 1, 3).reshape(B, S, D)
        out = out @ Wo + bo
        y = x + out
        mean = y.mean(axis=-1, keepdims=True)
        var = y.var(axis=-1, keepdims=True)
        y = (y - mean) * jax.lax.rsqrt(var + LN_EPS)
        return y * gamma + beta

    def _L3_ffn_ref(x, router_w, router_b, Wi, Wh, b, Wo, bo):
        import jax, jax.numpy as jnp
        import numpy as np
        S, B, I, O, H, E, K = (128, 32, 512, 512, 512, 8, 2)

        def _expert(x_seq, Wi, Wh, b, Wo, bo):
            Bsz = x_seq.shape[1]
            Hd = Wh.shape[0]

            def step(carry, xt):
                h, c = carry
                gates = xt @ Wi + h @ Wh + b
                i_, f_, g_, o_ = jnp.split(gates, 4, axis=-1)
                c = jax.nn.sigmoid(f_) * c + jax.nn.sigmoid(i_) * jnp.tanh(g_)
                h = jax.nn.sigmoid(o_) * jnp.tanh(c)
                return ((h, c), h @ Wo + bo)
            init = (jnp.zeros((Bsz, Hd), x_seq.dtype), jnp.zeros((Bsz, Hd), x_seq.dtype))
            _, ys = jax.lax.scan(step, init, x_seq)
            return ys
        S_, B_, I_ = x.shape
        N = S_ * B_
        flat_x = x.reshape(N, I_)
        logits = flat_x @ router_w + router_b
        top_vals, top_idx = jax.lax.top_k(logits, K)
        rw = jax.nn.softmax(top_vals, axis=1)
        mask = (top_idx.T[:, None, :] == jnp.arange(E)[None, :, None]).astype(x.dtype)
        expert_x = (mask[..., None] * flat_x[None, None]).reshape(K, E, S_, B_, I_)
        run_e = jax.vmap(_expert, in_axes=(0, 0, 0, 0, 0, 0))
        run_ke = jax.vmap(run_e, in_axes=(0, None, None, None, None, None))
        out = run_ke(expert_x, Wi, Wh, b, Wo, bo)
        out = out.reshape(K, E, N, -1)
        y = jnp.einsum('ken,nk,keno->no', mask, rw, out)
        return y.reshape(S_, B_, -1)
    edge_index = jnp.stack([src, dst])
    xn = _layernorm(x, axis=-1)
    x = x + _L0_gnn_ref(xn, edge_index, L0_gnn_Wl0, L0_gnn_bl0, L0_gnn_Wr0, L0_gnn_g0, L0_gnn_b0, L0_gnn_Wl1, L0_gnn_bl1, L0_gnn_Wr1, L0_gnn_g1, L0_gnn_b1, L0_gnn_Wl2, L0_gnn_bl2, L0_gnn_Wr2, L0_gnn_g2, L0_gnn_b2, L0_gnn_a_prelu) + _L0_mix_ref(xn[None], L0_mix_w_qkv, L0_mix_w_out, L0_mix_b_out)[0]
    x = x + _L0_ffn_ref(_layernorm(x, axis=-1)[None], L0_ffn_Wr0, L0_ffn_W1_0, L0_ffn_b1_0, L0_ffn_W2_0, L0_ffn_b2_0, L0_ffn_Wr1, L0_ffn_W1_1, L0_ffn_b1_1, L0_ffn_W2_1, L0_ffn_b2_1)[0]
    xn = _layernorm(x, axis=-1)
    x = x + _L1_gnn_ref(xn, src, dst, L1_gnn_W_self1, L1_gnn_W_neigh1, L1_gnn_b1, L1_gnn_W_self2, L1_gnn_W_neigh2, L1_gnn_b2) + _L1_mix_ref(xn[None], L1_mix_W_in, L1_mix_b_in, L1_mix_Wq, L1_mix_Wk, L1_mix_Wv, L1_mix_W_out, L1_mix_b_out)[0]
    x = x + _L1_ffn_ref(_layernorm(x, axis=-1)[None], L1_ffn_W_f, L1_ffn_b_f, L1_ffn_W_i, L1_ffn_b_i, L1_ffn_W_c, L1_ffn_b_c, L1_ffn_W_o, L1_ffn_b_o)[0]
    xn = _layernorm(x, axis=-1)
    x = x + _L2_gnn_ref(xn, edge_index, edge_attr_8, L2_gnn_Wq, L2_gnn_bq, L2_gnn_Wk, L2_gnn_bk, L2_gnn_Wv, L2_gnn_bv, L2_gnn_Wo, L2_gnn_bo) + _L2_mix_ref(xn[None], L2_mix_w_qkv, L2_mix_w_proj, L2_mix_b_proj)[0]
    x = x + _L2_ffn_ref(_layernorm(x, axis=-1)[None], L2_ffn_gate_w, L2_ffn_w1, L2_ffn_b1, L2_ffn_w2, L2_ffn_b2, L2_ffn_sw1, L2_ffn_sb1, L2_ffn_sw2, L2_ffn_sb2)[0]
    xn = _layernorm(x, axis=-1)
    x = x + _L3_gnn_ref(xn, edge_index, L3_gnn_W1, L3_gnn_b1, L3_gnn_W2, L3_gnn_b2, L3_gnn_Wg, L3_gnn_att_src, L3_gnn_att_dst, L3_gnn_bias_g, L3_gnn_W3, L3_gnn_b3) + _L3_mix_ref(xn[None], L3_mix_Wq, L3_mix_bq, L3_mix_Wk, L3_mix_bk, L3_mix_Wv, L3_mix_bv, L3_mix_Wo, L3_mix_bo, L3_mix_gamma, L3_mix_beta)[0]
    x = x + _L3_ffn_ref(_layernorm(x, axis=-1)[None], L3_ffn_router_w, L3_ffn_router_b, L3_ffn_Wi, L3_ffn_Wh, L3_ffn_b, L3_ffn_Wo, L3_ffn_bo)[0]
    return x

_drawn_inputs = setup_inputs


def setup_inputs(seed=0):
    import zlib

    import numpy as np

    out = dict(_drawn_inputs(seed))
    spreads = {'L0_gnn_bl0': (0.0, 0.1),
     'L0_gnn_g0': (1.0, 0.2),
     'L0_gnn_b0': (0.0, 0.1),
     'L0_gnn_bl1': (0.0, 0.1),
     'L0_gnn_g1': (1.0, 0.2),
     'L0_gnn_b1': (0.0, 0.1),
     'L0_gnn_bl2': (0.0, 0.1),
     'L0_gnn_g2': (1.0, 0.2),
     'L0_gnn_b2': (0.0, 0.1),
     'L1_gnn_b1': (0.0, 0.1),
     'L1_gnn_b2': (0.0, 0.1),
     'L1_mix_b_in': (0.0, 0.461),
     'L1_mix_b_out': (0.0, 0.1),
     'L2_gnn_bq': (0.0, 0.272),
     'L2_gnn_bk': (0.0, 2.0),
     'L2_gnn_bv': (0.0, 0.1),
     'L2_gnn_bo': (0.0, 0.1),
     'L3_gnn_b1': (0.0, 0.8),
     'L3_gnn_b2': (0.0, 0.8),
     'L3_gnn_bias_g': (0.0, 0.666),
     'L3_gnn_b3': (0.0, 0.8),
     'L3_mix_bq': (0.0, 2.0),
     'L3_mix_bk': (0.0, 2.0),
     'L3_mix_bv': (0.0, 2.0),
     'L3_mix_bo': (0.0, 2.0),
     'L3_mix_gamma': (1.0, 0.6),
     'L3_mix_beta': (0.0, 2.0),
     'L3_ffn_router_b': (0.0, 2.0),
     'L3_ffn_b': (0.0, 2.0),
     'L3_ffn_bo': (0.0, 2.0)}
    factors = {'L0_mix_b_out': 2.976,
     'L0_ffn_b1_0': 5.663,
     'L0_ffn_b2_0': 5.279,
     'L0_ffn_b1_1': 8.0,
     'L0_ffn_b2_1': 6.546,
     'L1_mix_W_in': 2.809,
     'L1_mix_Wq': 8.0,
     'L1_mix_Wk': 8.0,
     'L1_mix_Wv': 3.267,
     'L1_mix_W_out': 2.761,
     'L1_ffn_W_f': 2.883,
     'L1_ffn_b_f': 8.0,
     'L1_ffn_W_i': 2.682,
     'L1_ffn_b_i': 7.28,
     'L1_ffn_b_c': 3.535,
     'L1_ffn_b_o': 8.0,
     'L2_mix_b_proj': 5.189,
     'L2_ffn_b1': 8.0,
     'L2_ffn_b2': 8.0,
     'L2_ffn_sb1': 8.0,
     'L2_ffn_sb2': 8.0,
     'L3_gnn_W1': 8.0,
     'L3_gnn_W2': 8.0,
     'L3_gnn_Wg': 8.0,
     'L3_gnn_att_src': 8.0,
     'L3_gnn_att_dst': 8.0,
     'L3_gnn_W3': 4.293,
     'L3_mix_Wq': 200.0,
     'L3_mix_Wk': 200.0,
     'L3_ffn_Wi': 18.904,
     'L3_ffn_Wo': 17.348,
     'L3_mix_Wv': 3.0,
     'L3_mix_Wo': 2.932,
     'L3_ffn_router_w': 7.553}
    for name, (base, spread) in spreads.items():
        noise = np.random.default_rng([zlib.crc32(name.encode()), seed]).standard_normal(out[name].shape)
        drawn = base * np.exp(spread * noise) if base else spread * noise
        out[name] = jnp.asarray(drawn.astype(out[name].dtype))
    for name, factor in factors.items():
        out[name] = (out[name] * factor).astype(out[name].dtype)
    return out
```

```python
from contextlib import ExitStack

import concourse.bass as bass
from concourse import mybir

F32 = mybir.dt.float32
BF16 = mybir.dt.bfloat16
F16 = mybir.dt.float16
I32 = mybir.dt.int32
U32 = mybir.dt.uint32
ALU = mybir.AluOpType
ACT = mybir.ActivationFunctionType
AX_X = mybir.AxisListType.X

LAST = 8

DONE = {1: "L0.done", 2: "F1.y", 3: "L1.done", 4: "L1f.hs", 5: "L2.done", 6: "L2f.eo1", 7: "L3.done", 8: "L3f.y7"}

N = 625
NT = 5
R = N // NT
D = 512
KC = D // 128
E = 10000
ET = 80
EP = E // ET
H = 8
BIG = 1.0e30
RING = 4
LS_FILL = 8
SLOTS = 4

ROWS = {
    1: ["L0_gnn_bl0", "L0_gnn_g0", "L0_gnn_b0", "L0_gnn_bl1", "L0_gnn_g1", "L0_gnn_b1",
        "L0_gnn_bl2", "L0_gnn_g2", "L0_gnn_b2", "L0_mix_b_out"],
    2: ["L0_ffn_b1_0", "L0_ffn_b1_1"],
    3: ["L1_gnn_b1", "L1_gnn_b2", "L1_mix_b_out"],
    5: ["L2_gnn_bq", "L2_gnn_bk", "L2_gnn_bv", "L2_gnn_bo", "L2_mix_b_proj"],
    6: ["L2_ffn_sb2"],
    7: ["L3_gnn_b3", "L3_mix_bk", "L3_mix_bv", "L3_mix_bo", "L3_mix_gamma", "L3_mix_beta",
        "L3_gnn_bias_g", "L3_gnn_att_src", "L3_gnn_att_dst"],
    8: ["L3_ffn_router_b"],
}
ROW_HALVES = sorted(ROWS)
NROWS = max(len(x) for x in ROWS.values())
EBIAS = {2: ["L0_ffn_b2_0", "L0_ffn_b2_1"], 6: ["L2_ffn_b2"], 8: ["L3_ffn_bo"]}

COLS = [("L1_mix_b_in", 4), ("L1_ffn_b_f", 4), ("L1_ffn_b_i", 4), ("L1_ffn_b_o", 4), ("L1_ffn_b_c", 4),
        ("L2_ffn_b1", 8), ("L2_ffn_sb1", 4), ("L3_gnn_b1", 2), ("L3_gnn_b2", 4), ("L3_mix_bq", 4),
        ("L3_ffn_b", 128), ("a_prelu", 1)]
COL_AT, _n = {}, 0
for _name, _k in COLS:
    COL_AT[_name] = _n
    _n += _k
NCOLS = _n

WEIGHTS = [
    ("L0_gnn_Wl0", 4, 512, "L0.conv0"), ("L0_gnn_Wr0", 4, 512, "L0.conv0"),
    ("L0_wq", 4, 512, "L0.q"), ("L0_wk", 4, 512, "L0.k"), ("L0_wv", 4, 512, "L0.v"),
    ("L0_gnn_Wl1", 4, 512, "L0.conv1"), ("L0_gnn_Wr1", 4, 512, "L0.conv1"),
    ("L0_gnn_Wl2", 4, 512, "L0.conv2"), ("L0_gnn_Wr2", 4, 512, "L0.conv2"),
    ("L0_wo", 4, 512, "L0.out"),
    ("L0_ffn_W1_0", 4, 256, "F0.h"), ("L0_ffn_W2_0", 2, 512, "F0.y"),
    ("L0_ffn_W1_1", 4, 512, "F1.h"), ("L0_ffn_W2_1", 4, 512, "F1.y"),
    ("L1_gnn_W_self1", 4, 512, "L1.g0"), ("L1_gnn_W_neigh1", 4, 512, "L1.g0"),
    ("L1_mix_W_in", 4, 512, "L1.xm"),
    ("L1_gnn_W_self2", 4, 512, "L1.g1"), ("L1_gnn_W_neigh2", 4, 512, "L1.g1"),
    ("L1_mix_W_out", 4, 512, "L1.out"),
    ("L1_wh_i", 4, 512, "split0"), ("L1_wh_f", 4, 512, "split1"),
    ("L1_wh_o", 4, 512, "split2"), ("L1_wh_c", 4, 512, "split3"),
    ("L1_wx_i", 4, 512, "L1f.gx0"), ("L1_wx_f", 4, 512, "L1f.gx1"),
    ("L1_wx_o", 4, 512, "L1f.gx2"), ("L1_wx_c", 4, 512, "L1f.gx3"),
    ("L2_gnn_Wq", 4, 512, "L2.gq"), ("L2_gnn_Wk", 4, 512, "L2.gk"), ("L2_gnn_Wv", 4, 512, "L2.gv"),
    ("L2_wq", 4, 512, "L2.q"), ("L2_wk", 4, 512, "L2.k"), ("L2_wv", 4, 512, "L2.v"),
    ("L2_wo", 4, 512, "L2.out"), ("L2_gnn_Wo", 4, 512, "L2.gout"),
    ("L2_ffn_sw1", 4, 512, "L2f.s1"), ("L2_ffn_sw2", 4, 512, "L2f.s2"),
    ("L2_w1_0", 4, 512, "L2f.h0"), ("L2_w1_1", 4, 512, "L2f.h1"),
    ("L2_w2_0", 4, 512, "L2f.eo0"), ("L2_w2_1", 4, 512, "L2f.eo1"),
    ("L3_gnn_W1", 4, 256, "L3.x1"), ("L3_gnn_W2", 2, 512, "L3.x2"), ("L3_gnn_Wg", 4, 256, "L3.xp"),
    ("L3_gnn_W3", 2, 512, "L3.gout"),
    ("L3_wq", 4, 512, "L3.q"), ("L3_wk", 4, 512, "L3.k"), ("L3_wv", 4, 512, "L3.v"),
    ("L3_wo", 4, 512, "L3.out"),
]
for _e in range(9):
    if _e < 8:
        WEIGHTS += [(f"L3_wi{_e}", 4, 512, f"L3f.i{_e}"), (f"L3_wg{_e}", 4, 512, f"L3f.g{_e}"),
                    (f"L3_wo_{_e}", 4, 512, f"L3f.o{_e}")]
    if _e:
        WEIGHTS += [(f"L3_wout{_e - 1}", 4, 512, f"L3f.y{_e - 1}")]

TILES = [
    ("pre.cnt", 1, "V", 1),
    ("L0.xnT", 5, "A", 1), ("L0.agg0", 4, "A", 1), ("L0.conv0", 5, "V", 1),
    ("L0.q", 4, "A", 1), ("L0.k", 5, "A", 1), ("L0.v", 5, "A", 1),
    ("L0.hT0", 5, "A", 1), ("L0.agg1", 4, "A", 1), ("L0.conv1", 5, "V", 1),
    ("L0.ctx", 2, "V", 1), ("L0.den", 1, "V", 1), ("L0.num", 5, "V", 1),
    ("L0.hT1", 5, "A", 1), ("L0.agg2", 4, "A", 1), ("L0.conv2", 5, "V", 1),
    ("L0.oT", 5, "A", 1), ("L0.out", 5, "V", 1),
    ("L0f.xnT", 5, "A", 2), ("F0.lg", 1, "V", 2), ("F0.pT", 1, "A", 2), ("F0.h", 5, "V", 2),
    ("F0.hT", 5, "A", 2), ("F0.y", 5, "A", 2), ("F1.xT", 5, "A", 2),
    ("F1.lg", 1, "V", 2), ("F1.pT", 1, "A", 2), ("F1.h", 5, "V", 2), ("F1.hT", 5, "A", 2), ("F1.y", 5, "V", 2),
    ("L1.xnT", 5, "A", 3), ("L1.agg0", 4, "A", 3), ("L1.g0", 5, "V", 3), ("L1.xm", 4, "A", 3),
    ("L1.mq", 5, "V", 3), ("L1.mk", 2, "A", 3), ("L1.mv", 5, "A", 3),
    ("L1.hT", 5, "A", 3), ("L1.agg1", 4, "A", 3), ("L1.g1", 5, "V", 3),
    ("L1.qT", 5, "A", 3), ("L1.kR", 5, "A", 3), ("L1.kv", 1, "V", 3), ("L1.num", 5, "A", 3),
    ("L1.oT", 5, "A", 3), ("L1.out", 5, "V", 3),
    ("L1f.xnT", 5, "A", 4), ("sort.deg", 1, "V", 4), ("L1f.gx0", 4, "A", 4), ("L1f.gx1", 4, "A", 4), ("L1f.gx2", 4, "A", 4),
    ("L1f.gx3", 4, "A", 4), ("L1f.hs", 5, "V", 4),
    ("L2.xnT", 5, "A", 5), ("L2.gq", 5, "V", 5), ("L2.gk", 5, "V", 5), ("L2.gv", 5, "V", 5),
    ("L2.q", 4, "A", 5), ("L2.k", 5, "A", 5), ("L2.v", 5, "A", 5),
    ("L2.ctx", 2, "V", 5), ("L2.den", 1, "V", 5), ("L2.num", 5, "V", 5), ("L2.oT", 5, "A", 5), ("L2.out", 5, "V", 5),
    ("L2.lT", 20, "A", 5), ("L2.fT", 20, "V", 5), ("L2.mR", 2, "V", 5),
    ("L2.yT", 5, "A", 5), ("L2.gout", 5, "V", 5),
    ("L2f.xnT", 5, "A", 6), ("L2f.lg", 1, "V", 6), ("L2f.s1", 4, "A", 6), ("L2f.cT", 1, "A", 6), ("L2f.s2", 5, "V", 6),
    ("L2f.h0", 4, "A", 6), ("L2f.h1", 4, "A", 6), ("L2f.eo0", 20, "V", 6), ("L2f.eo1", 20, "V", 6),
    ("L3.xnT", 5, "A", 7), ("L3.x1", 2, "A", 7), ("L3.x2", 4, "A", 7), ("L3.xp", 5, "A", 7),
    ("L3.adjT", 5, "V", 7), ("L3.sdB", 4, "A", 7), ("L3.mxB", 2, "A", 7), ("L3.gat", 5, "V", 7),
    ("L3.gT", 5, "A", 7), ("L3.gout", 5, "V", 7),
    ("L3.q", 4, "A", 7), ("L3.k", 5, "V", 7), ("L3.v", 5, "V", 7),
    ("L3.ctx", 2, "V", 7), ("L3.den", 1, "V", 7), ("L3.num", 5, "V", 7), ("L3.oT", 5, "A", 7), ("L3.out", 5, "V", 7),
    ("L3f.xnT", 5, "A", 8), ("L3f.lg", 1, "V", 8), ("L3f.cT", 1, "A", 8), ("L3f.b", 5, "V", 8),
]
for _e in range(9):
    if _e < 8:
        TILES += [(f"L3f.i{_e}", 4, "A", 8), (f"L3f.g{_e}", 4, "A", 8), (f"L3f.o{_e}", 4, "A", 8)]
    if _e:
        TILES += [(f"L3f.y{_e - 1}", 5, "V", 8)]

MADE = [
    ("pre.consts", 1, 1), ("sort.consts", 1, 4),
    ("L0.qmin", 4, 1), ("L0.kmin", 5, 1),
    ("L2.qmin", 4, 5), ("L2.kmin", 5, 5), ("L3.qmin", 4, 7), ("L3.kmin", 5, 7),
    ("L0.qexp", 4, 1), ("L0.kexp", 5, 1), ("L2.qexp", 4, 5), ("L2.kexp", 5, 5), ("L3.qexp", 4, 7), ("L3.kexp", 5, 7),
    ("F0.pexp", 1, 2), ("F1.pexp", 1, 2), ("L1.pexp", 5, 3), ("L1.kexps", 2, 3), ("L2.pexp", 1, 5), ("L2f.pexp", 1, 6),
    ("L3.pexp", 10, 7), ("L3f.pexp", 1, 8),
    ("pre.ids", 1, 1), ("pre.counts", 5, 1), ("pre.agg", 5, 1),
    ("L0.xn", 5, 1), ("L0f.xn", 5, 2), ("L1.xn", 5, 3), ("L1f.xn", 5, 4), ("L2.xn", 5, 5), ("L2f.xn", 5, 6),
    ("L3.xn", 5, 7), ("L3f.xn", 5, 8),
    ("L0.h0", 5, 1), ("L0.h1", 5, 1), ("L1.h", 5, 3),
    ("L0.qfm", 4, 1), ("L0.kfm", 5, 1), ("L2.qfm", 4, 5), ("L2.kfm", 5, 5), ("L3.qfm", 4, 7), ("L3.kfm", 5, 7),
    ("L0.ctxd", 8, 1), ("L2.ctxd", 8, 5), ("L3.ctxd", 8, 7),
    ("F0.sub", 1, 2), ("F0.prob", 1, 2), ("F0.hw", 5, 2), ("F1.sub", 1, 2), ("F1.prob", 1, 2), ("F1.hw", 5, 2),
    ("L1.qs", 5, 3), ("L1.kneg", 1, 3), ("L1.ks", 2, 3), ("L1.kvd", 3, 3),
    ("sort.srcdeg", 1, 4), ("L1f.split", 4, 4), ("L1f.halfbias", 1, 4), ("sort.offs", 1, 4), ("sort.place", 1, 4), ("sort.table", 1, 4),
    ("L2f.sub", 1, 6), ("L2f.prob", 1, 6),
    ("L3.selfs", 5, 7), ("L3.sd", 10, 7), ("L3.onec", 1, 7), ("L3.mx", 1, 7), ("L3.sub", 10, 7), ("L3.pt", 10, 7), ("L3.og", 5, 7),
    ("L3f.sub", 1, 8), ("L3f.prob", 1, 8),
    ("L0.done", 5, 1), ("L1.done", 5, 3), ("L2.done", 5, 5), 
    ("L3.done", 5, 7), 
    ("L2.logit", 1, 5), ("L2.flag", 1, 5), ("L2.rowmax", 1, 5), ("L2.ysum", 5, 5), ("L2.idx", 1, 5),
]
for _e in range(8):
    MADE += [(f"L3f.cell{_e}", 1, 8), (f"L3f.tc{_e}", 1, 8), (f"L3f.hid{_e}", 1, 8)]


def kind_of(name):
    return name.split(".")[1].rstrip("0123456789")


def network(nc, io, last):
    tiles = [t for t in TILES if t[3] <= last]
    first, evac_at, evacs = {}, {}, {"A": 0, "V": 0}
    g = 0
    for name, k, who, _ in tiles:
        first[name] = (g, k)
        for i in range(k):
            evacs[who] += 1
            evac_at[g + i] = (who, evacs[who])
        g += k
    made_at, made_n = {}, {}
    for name, k, half in MADE:
        if half <= last:
            kind = kind_of(name)
            made_at[name] = made_n.get(kind, 0)
            made_n[kind] = made_n.get(kind, 0) + k
    halves = {t[0]: t[3] for t in TILES}
    weights = [w for w in WEIGHTS if (4 if w[3].startswith("split") else halves[w[3]]) <= last]
    weight_at = {w[0]: n for n, w in enumerate(weights)}

    with ExitStack() as ctx:
        def sb(name, shape, dt=F32):
            return ctx.enter_context(nc.sbuf_tensor(name, shape, dt))

        def sem(name):
            return ctx.enter_context(nc.semaphore(name))

        PS = ctx.enter_context(nc.psum_tensor("PS", [128, SLOTS, 1024], F32))
        PSF = PS[:, :, :].rearrange("p s n -> p (s n)")
        ring = sb("ring", [128, RING, 2048])
        BUF = sb("BUF", [128, 10 * 2560])
        X = sb("X", [128, NT, D])
        AC = sb("AC", [128, NT, N])
        AH = sb("AH", [128, NT, N])
        rows = sb("rows", [128, NROWS, D])
        cols = sb("cols", [128, NCOLS])
        ident = sb("ident", [128, 128])
        ones = sb("ones", [128, 128])
        iota = sb("iota", [128, N])
        rev8 = sb("rev8", [128, 8])
        wr = sb("wr", [128, 4, 4, 8])
        ids = sb("ids", [128, 2, ET])
        ctxd = sb("ctxd", [128, 4, 128])
        ksd = sb("ksd", [128, 4, 8])
        duo = sb("duo", [128, 960])
        bdq = duo[:, 0:64]
        bdk = duo[:, 64:320].rearrange("p (c n) -> p c n", c=2)
        bdv = duo[:, 320:448]
        kvd = duo[:, 448:960].rearrange("p (c n) -> p c n", c=2)
        stats = sb("stats", [128, NT, 6])
        mv = sb("mv", [128, NT, 2])
        nw = sb("nw", [128, 4, NT])
        nwi = sb("nwi", [128, NT], I32)
        sm = sb("sm", [128, 12, NT, 8])
        smr = sb("smr", [128, 6, NT, 8])
        den = sb("den", [128, NT, 8])
        small = sb("small", [128, 64])
        ls_parts = sb("ls_parts", [128, KC, 32], BF16)
        ls_act = sb("ls_act", [128, 16])
        ls_gate = sb("ls_gate", [128, 20])
        ls_pr = sb("ls_pr", [128, 8])
        ls_2c = sb("ls_2c", [128, 4])
        ls_th = sb("ls_th", [128, 4])
        ls_rest = sb("ls_rest", [128, 4])
        ls_h2 = sb("ls_h2", [128, 4])

        def B(n, count=1):
            return BUF[:, n * 2560:(n + count) * 2560]

        def rowsof(ap, w=D):
            return ap[0:R, 0:NT * w].rearrange("p (t f) -> p t f", t=NT)

        def colsof(ap, k=KC):
            return ap[:, 0:k * N].rearrange("p (c n) -> p c n", c=k)

        tile_full = sem("tile_full")
        evac = {"A": sem("evacuated_by_act"), "V": sem("evacuated_by_dve")}
        made_sem = {kind: sem(kind + "_ready") for kind in made_n}
        weight_in = [sem(f"weight_in{s}") for s in range(RING)]
        consts_in = sem("consts_in")
        blocks_in = sem("blocks_in")
        x_in = sem("x_in")
        edges_in = sem("edges_in")
        rows_in = sem("rows_in")
        ebias_in = sem("ebias_in")
        out_done = sem("out_done")
        dve_step = sem("dve_step")
        act_step = sem("act_step")
        pool_step = sem("pool_step")
        l1_hot = sem("l1_hot")
        l1_used = sem("l1_used")
        ls_full = sem("ls_full")
        ls_pre = sem("ls_pre")
        ls_sig = sem("ls_sig")
        ls_cell = sem("ls_cell")
        ls_tanh = sem("ls_tanh")
        ls_h = sem("ls_h")
        ls_part = sem("ls_part")
        rk_hot = sem("rk_hot")
        rk_seen = sem("rk_seen")
        rk_cum = sem("rk_cum")
        rk_pos = sem("rk_pos")
        rk_put = sem("rk_put")
        attr_in = sem("attr_in")
        pad_out = sem("pad_out")
        staged = sem("staged")
        sent = sem("sent")
        scattered = [sem("scattered0"), sem("scattered1")]
        qkv_out = sem("qkv_out")
        sorted_in = sem("sorted_in")
        qk_staged = sem("qk_staged")
        qk_in = [sem(f"qk_in{u}") for u in range(4)]
        qk_used = sem("qk_used")
        qk_prod = sem("qk_prod")
        v_staged = sem("v_staged")
        v_in = [sem("v_in0"), sem("v_in1")]
        v_used = sem("v_used")
        pv_ready = sem("pv_ready")
        pv_used = sem("pv_used")

        sorted_d = nc.dram_tensor("sorted_edges", (E + 1, 10), F32).ap()
        q_d = nc.dram_tensor("q_nodes", (N, D), F32).ap()
        k_d = nc.dram_tensor("k_nodes", (N, D), F32).ap()
        v_d = nc.dram_tensor("v_nodes", (N, D), F32).ap()

        block = ctx.enter_context(nc.Block())

        def full(stage, i):
            return tile_full, first[stage][0] + i + 1

        def evacd(stage, i=None):
            g0, k = first[stage]
            who, n = evac_at[g0 + (k - 1 if i is None else i)]
            return evac[who], n

        def made(name, n=None):
            kind = kind_of(name)
            k = [m[1] for m in MADE if m[0] == name][0]
            return made_sem[kind], made_at[name] + (k if n is None else n)

        def slot(stage, i):
            return PS[:, (first[stage][0] + i) % SLOTS, :]

        def bank(stage, i):
            return slot(stage, i)[:, 0:512]

        def half_done(half):
            return evacd(DONE[half]) if DONE[half] in first else made(DONE[half])

        def rows_ready(half):
            return rows_in, 16 * (ROW_HALVES.index(half) + 1)

        def ebias_ready(half):
            return ebias_in, 16 * (sorted(EBIAS).index(half) + 1)

        emitted = {}

        def make(ins, name):
            emitted[name] = emitted.get(name, 0) + 1
            ins.then_inc(made_sem[kind_of(name)], 1)

        def took(ins, stage, i):
            emitted[stage] = emitted.get(stage, 0) + 1
            assert emitted[stage] == i + 1
            ins.then_inc(evac[evac_at[first[stage][0] + i][0]], 1)

        def weight(name):
            n = weight_at[name]
            _, k, w, _ = weights[n]
            return ring[:, n % RING, 0:k * w].rearrange("p (k w) -> p k w", k=k)

        def weight_ready(name):
            n = weight_at[name]
            return weight_in[n % RING], 16 * (n // RING + 1)

        class Steps:
            def __init__(self, eng, s):
                self.eng, self.sem, self.n = eng, s, 0

            def done(self, ins):
                self.n += 1
                ins.then_inc(self.sem, 1)
                return self.n

            def after(self, n=None):
                self.eng.wait_ge(self.sem, self.n if n is None else n)

        xn, xnT = rowsof(B(0)), colsof(B(1))
        qT, kR, vR, tmpB = colsof(B(6)), rowsof(B(7)), rowsof(B(8)), B(9)
        oR, oT = rowsof(B(9)), colsof(B(7))
        lnbuf = rowsof(B(5))
        eb = B(8)[0:8, 0:2 * D].rearrange("p (a b) -> p a b", a=2)
        combT = B(9)[0:8, 0:N]
        src_i = B(5)[:, 0:2 * ET].bitcast(I32).rearrange("p (a b) -> p a b", a=2)
        rw = rows[:, :, :].rearrange("p a b -> p (a b)")
        ah = AH[:, :, :].rearrange("p a b -> p (a b)")
        cnt_src, offs, zeros = (rw[0:R, 640 * j:640 * j + N] for j in range(3))
        offs_i = rw[0:R, 1920:1920 + N].bitcast(I32)
        b7 = rw[:, 2560:4608].bitcast(BF16)
        offs_hi, offs_lo = b7[0:EP, 0:N], b7[0:EP, 1024:1024 + N]
        tri, oneb, row0 = b7[0:EP, 2048:2048 + EP], b7[0:EP, 2304:2304 + EP], b7[0:EP, 2560:2560 + EP]
        b6 = ah.bitcast(BF16)
        hot_rank = [b6[0:EP, 640 * u:640 * u + N] for u in range(2)]
        seen = [b6[0:EP, 640 * (2 + u):640 * (2 + u) + N] for u in range(2)]
        junk = [b6[0:EP, 640 * (4 + u):640 * (4 + u) + N] for u in range(2)]
        attr = ah[:, 1920:1920 + 8 * ET]
        place_f = ah[:, 2560:2560 + ET]
        place = duo[:, 10 * ET:11 * ET].bitcast(U32)
        table = duo[:, 0:10 * ET].rearrange("p (t c) -> p t c", c=10)
        sorted_e = ah[:, 0:10 * (ET + 1)].rearrange("p (t c) -> p t c", c=10)
        eidx = ah[:, 832:832 + 2 * ET].bitcast(U32).rearrange("p (j t) -> p j t", j=2)
        logit = ah[:, 1024:1024 + H * ET].rearrange("p (t h) -> p t h", h=H)
        flag = ah[:, 1728:1728 + ET]
        idx_stage = sb("idx_stage", [128, 8], U32)
        row_stage = sb("row_stage", [128, 2, 10])
        frow = B(2, 2).bitcast(BF16)[0:8, 0:E + 1]
        lrow = B(4, 4)[0:8, 0:E]
        gat_q = [B(2, 2)[0:EP, 1024 * u:1024 * u + 512] for u in range(4)]
        gat_k = [B(2, 2)[0:EP, 1024 * u + 512:1024 * u + 1024] for u in range(4)]
        prod = B(8)[0:EP, 2048:2560]
        gat_v = [B(9)[0:EP, 520 * u:520 * u + 512] for u in range(2)]
        pv = [B(9)[0:EP, 520 * (2 + u):520 * (3 + u)] for u in range(2)]
        hot_s = [B(0)[0:EP, 640 * u:640 * u + N] for u in range(2)]
        zero5 = B(1)[:, 0:512]
        h1T = B(3, 2)[:, 0:8 * N].rearrange("p (c n) -> p c n", c=8)
        xp = B(4)[0:R, 0:NT * 258].rearrange("p (t h f) -> p t h f", t=NT, h=2)
        sB = B(5)[0:R, 0:4 * N].rearrange("p (j n) -> p j n", j=4)
        mB = B(2)[0:R, 0:2 * N].rearrange("p (j n) -> p j n", j=2)
        pT = B(6, 3)[0:R, 0:10 * N].rearrange("p (j n) -> p j n", j=10)
        og = rowsof(B(5), 256)
        sd = sb("sd", [128, 4, NT])
        mxc = sb("mxc", [128, 2, NT])
        lx = AH[:, :, :].rearrange("p a b -> p (a b)")[:, 0:KC * N].rearrange("p (c n) -> p c n", c=KC)
        ls_out = colsof(B(0))
        ls_w = BUF[:, 2560:2560 + 12288].bitcast(BF16).rearrange("p (s j c n) -> p s j c n", s=3, j=4, c=KC)
        ls_turn = BUF[:, 2560 + 12288:2560 + 12800]
        ls_gx = BUF[:, 6 * 2560:6 * 2560 + 16 * N].rearrange("p (g n) -> p g n", g=16)
        ls_sum = PS[:, 0, 0:512]

        @block.sync
        def _(sp):
            with nc.allow_non_contiguous_dma("layouts"):
                sp.dma_start(src_i[0:EP, :, :], io["edges"]).then_inc(edges_in, 16)
                sp.dma_start(X[0:R, :, :], io["x"].rearrange("(t p) f -> p t f", p=R)).then_inc(x_in, 16)
                sp.dma_start(cols[:, :], io["cols"]).then_inc(consts_in, 16)
                sp.dma_start(wr[:, :, :, :], io["routers"]).then_inc(consts_in, 16)

                for n, (name, k, w, user) in enumerate(weights):
                    if n >= RING:
                        old = weights[n - RING][3]
                        if old.startswith("split"):
                            sp.wait_ge(*made("L1f.split", int(old[5:]) + 1))
                        else:
                            sp.wait_ge(*full(old, first[old][1] - 1))
                    sp.dma_start(ring[:, n % RING, 0:k * w].rearrange("p (k w) -> p k w", k=k),
                                 io[name]).then_inc(weight_in[n % RING], 16)

            sp.wait_ge(*half_done(last))
            sp.dma_start(io["out"].rearrange("(t p) f -> p t f", p=R), X[0:R, :, :]).then_inc(out_done, 16)
            sp.wait_ge(out_done, 16)

        @block.gpsimd
        def _(pool):
            st = Steps(pool, pool_step)
            st.done(nc.gpsimd.memset(ident[:, :], 0.0))
            st.done(nc.gpsimd.memset(ones[:, :], 1.0))
            st.done(nc.gpsimd.memset(row_stage[0:1, 0, :], -1.0))
            st.done(nc.gpsimd.memset(ctxd[:, :, :], 0.0))
            st.done(nc.gpsimd.memset(ksd[:, :, :], 0.0))
            st.done(nc.gpsimd.iota(iota[:, :], [[1, N]], base=0, channel_multiplier=0,
                                   allow_small_or_imprecise_dtypes=True))
            st.done(nc.gpsimd.iota(rev8[:, :], [[-1, 8]], base=8, channel_multiplier=0,
                                   allow_small_or_imprecise_dtypes=True))
            st.after()
            pool.dma_start(sorted_d[0:1, :], row_stage[0:1, 0, :]).then_inc(pad_out, 16)
            make(nc.gpsimd.affine_select(out=ident[:, :], in_=ident[:, :], compare_op=ALU.not_equal, fill=1.0,
                                         base=0, pattern=[[-1, 128]], channel_multiplier=1), "pre.consts")

            def mins(layer):
                tq, tk = colsof(tmpB), rowsof(tmpB)
                for c in range(KC):
                    pool.wait_ge(*evacd(layer + ".q", c))
                    make(nc.gpsimd.tensor_scalar(tq[:, c, :], qT[:, c, :], 0.0, None, ALU.min), layer + ".qmin")
                pool.wait_ge(*made(layer + ".qfm"))
                for t in range(NT):
                    pool.wait_ge(*evacd(layer + ".k", t))
                    make(nc.gpsimd.tensor_scalar(tk[:, t, :], kR[:, t, :], 0.0, None, ALU.min), layer + ".kmin")

            def load_rows(half):
                if half > 1:
                    pool.wait_ge(*half_done(half - 1))
                k = len(ROWS[half]) * D
                j = ROW_HALVES.index(half)
                pool.dma_start(rows[:, :, :].rearrange("p a b -> p (a b)")[:, 0:k],
                               io["rows"][j:j + 1, 0:k].to_broadcast([128, k])).then_inc(rows_in, 16)
                if half in EBIAS:
                    j = sorted(EBIAS).index(half)
                    pool.dma_start(eb[:, :, :], io["ebias"][j]).then_inc(ebias_in, 16)

            load_rows(1)
            rk = nc.gpsimd
            mins("L0")
            if last >= 2:
                load_rows(2)
            if last >= 3:
                st.done(nc.gpsimd.memset(duo[:, :], 0.0))
                st.after()
                with nc.allow_non_contiguous_dma("blocks"):
                    for h in range(2):
                        p = 64 * h
                        pool.dma_start(bdq[p:p + 64, 32 * h:32 * h + 32], io["L1_mix_Wq"]).then_inc(blocks_in, 16)
                        for c in range(2):
                            pool.dma_start(bdk[p:p + 64, c, 64 * c + 32 * h:64 * c + 32 * h + 32],
                                           io["L1_mix_Wk"]).then_inc(blocks_in, 16)
                        pool.dma_start(bdv[p:p + 64, p:p + 64], io["L1_mix_Wv"]).then_inc(blocks_in, 16)
                load_rows(3)
            if last >= 4:
                pool.wait_ge(*half_done(3))
                st.done(nc.gpsimd.memset(oneb, 1.0))
                st.done(nc.gpsimd.memset(tri, 1.0))
                st.done(nc.gpsimd.memset(row0, 0.0))
                st.after()
                st.done(nc.gpsimd.memset(row0[0:1, :], 1.0))
                st.done(nc.gpsimd.affine_select(out=tri, in_=tri, compare_op=ALU.is_gt, fill=0.0, base=0,
                                                pattern=[[1, EP]], channel_multiplier=-1))
                pool.wait_ge(*evacd("L1f.gx3"))
                pool.dma_start(attr[0:EP, :], io["attr"]).then_inc(attr_in, 16)
                st.after()
                make(nc.gpsimd.memset(seen[0], 0.0), "sort.consts")
                pool.wait_ge(*made("sort.consts"))
                pool.sem_inc(rk_seen, 1)
                with pool.Fori(0, ET // 2) as it:
                    for u in range(2):
                        pool.wait_ge(rk_hot, it * 2 + (u + 1))
                        pool.wait_ge(rk_cum, it * 2 + (u + 1))
                        pool.wait_ge(rk_seen, it * 2 + (u + 1))
                        rk.tensor_tensor(seen[1 - u], seen[u], hot_rank[u], ALU.add).then_inc(rk_seen, 1)
                pool.wait_ge(pad_out, 16)
                pool.wait_ge(*made("sort.place"))
                pool.wait_ge(*made("sort.table"))

                def scatter(it, u):
                    rk.tensor_copy(idx_stage[0:EP, u:u + 1], place[0:EP, bass.ds(it * 2 + u, 1)]).then_inc(staged, 1)
                    rk.tensor_copy(row_stage[0:EP, u, :], table[0:EP, bass.ds(it * 2 + u, 1), :]).then_inc(staged, 1)
                    pool.wait_ge(staged, it * 4 + (2 * u + 2))
                    pool.sem_inc(sent, 1)
                    pool.indirect_dma_start(sorted_d, bass.IndirectOffsetOnAxis(ap=idx_stage[0:EP, u:u + 1], axis=0),
                                            row_stage[0:EP, u, :], None).then_inc(scattered[u], 16)
                for u in range(2):
                    scatter(0, u)
                with pool.Fori(1, ET // 2) as it:
                    for u in range(2):
                        pool.wait_ge(scattered[u], it * 16)
                        scatter(it, u)
            if last >= 5:
                load_rows(5)
                for u in range(2):
                    pool.wait_ge(scattered[u], 8 * ET)
                pool.dma_start(sorted_e[0:EP, 1:ET + 1, :],
                               sorted_d[1:E + 1, :].rearrange("(p t) c -> p t c", t=ET)).then_inc(sorted_in, 16)
                with nc.allow_non_contiguous_dma("one row of each partition"):
                    pool.dma_start(sorted_e[0:EP, 0, :],
                                   sorted_d[0:E, :].rearrange("(p t) c -> p t c", t=ET)[:, 0, :]).then_inc(sorted_in, 16)
                for dst, b, stage in ((q_d, 2, "L2.gq"), (k_d, 3, "L2.gk"), (v_d, 4, "L2.gv")):
                    pool.wait_ge(*evacd(stage))
                    pool.dma_start(dst.rearrange("(t p) f -> p t f", p=R), rowsof(B(b))).then_inc(qkv_out, 16)
                mins("L2")
                pool.wait_ge(qkv_out, 48)
                pool.wait_ge(*made("L2.idx"))

                def gather_qk(it, u):
                    for j in range(2):
                        rk.tensor_copy(idx_stage[0:EP, 2 * u + j:2 * u + j + 1],
                                       eidx[0:EP, j, bass.ds(it * 4 + u, 1)]).then_inc(qk_staged, 1)
                    pool.wait_ge(qk_staged, it * 8 + (2 * u + 2))
                    pool.sem_inc(sent, 1)
                    for j, (to, of) in enumerate(((gat_q, q_d), (gat_k, k_d))):
                        pool.indirect_dma_start(to[u], None, of, bass.IndirectOffsetOnAxis(
                            ap=idx_stage[0:EP, 2 * u + j:2 * u + j + 1], axis=0)).then_inc(qk_in[u], 16)
                for u in range(4):
                    gather_qk(0, u)
                with pool.Fori(1, ET // 4) as it:
                    for u in range(4):
                        pool.wait_ge(qk_in[u], it * 32)
                        pool.wait_ge(qk_used, it * 4 + (u - 3))
                        gather_qk(it, u)

                def gather_v(it, u):
                    rk.tensor_copy(idx_stage[0:EP, 2 * u:2 * u + 1],
                                   eidx[0:EP, 1, bass.ds(it * 2 + u, 1)]).then_inc(v_staged, 1)
                    pool.wait_ge(v_staged, it * 2 + (u + 1))
                    pool.sem_inc(sent, 1)
                    pool.indirect_dma_start(gat_v[u], None, v_d, bass.IndirectOffsetOnAxis(
                        ap=idx_stage[0:EP, 2 * u:2 * u + 1], axis=0)).then_inc(v_in[u], 16)
                for u in range(4):
                    pool.wait_ge(qk_in[u], 8 * ET)
                pool.wait_ge(*made("L2.logit"))
                for u in range(2):
                    gather_v(0, u)
                with pool.Fori(1, ET // 2) as it:
                    for u in range(2):
                        pool.wait_ge(v_in[u], it * 16)
                        pool.wait_ge(v_used, it * 2 + (u - 1))
                        gather_v(it, u)
            if last >= 6:
                load_rows(6)
            if last >= 7:
                load_rows(7)
                mins("L3")
            if last >= 8:
                load_rows(8)

        @block.tensor
        def _(pe):
            def begin(stage, i):
                g = first[stage][0] + i
                if g >= SLOTS:
                    who, n = evac_at[g - SLOTS]
                    pe.wait_ge(evac[who], n)
                return slot(stage, i)

            def mm_all(out, terms, stop_inc=True):
                for j, (a, b) in enumerate(terms):
                    ins = nc.tensor.matmul(out, a, b, start=(j == 0), stop=(j == len(terms) - 1))
                return ins

            def rows_stage(stage, terms, w=D):
                for t in range(NT):
                    o = begin(stage, t)
                    mm_all(o[0:R, 0:w], terms(t)).then_inc(tile_full, 1)

            def halves_stage(stage, c, terms, parts=128):
                o = begin(stage, c)
                for a, b in ((0, 512), (512, N)):
                    ins = mm_all(o[0:parts, a:b], terms(a, b))
                ins.then_inc(tile_full, 1)

            def dense_rows(stage, pairs, k=KC, w=D, extra=None):
                rows_stage(stage, lambda t: [(a[:, c, t * R:(t + 1) * R], b[:, c, 0:w]) for a, b in pairs
                                             for c in range(k)] + (extra(t) if extra else []), w)

            def dense_cols(stage, a, b, outs, k=KC):
                for o in range(outs):
                    halves_stage(stage, o, lambda lo, hi: [(b[:, c, 128 * o:128 * o + 128], a[:, c, lo:hi])
                                                           for c in range(k)])

            def turn_rows(stage, a, ready, k=KC):
                for t in range(NT):
                    o = begin(stage, t)
                    ready(t)
                    for c in range(k):
                        ins = nc.tensor.transpose(o[:, c * R:(c + 1) * R], a[:, t, 128 * c:128 * c + 128],
                                                  ident[0:R, 0:R])
                    ins.then_inc(tile_full, 1)

            def aggregate(stage, h):
                for c in range(KC):
                    halves_stage(stage, c, lambda lo, hi: [(h[:, t, 128 * c:128 * c + 128], AH[0:R, t, lo:hi])
                                                           for t in range(NT)])

            def attention(L):
                for j in range(2):
                    o = begin(L + ".ctx", j)
                    for q in range(2):
                        p = 2 * j + q
                        mm_all(o[:, 129 * q:129 * q + 128],
                               [(kR[:, t, 128 * p:128 * p + 128], vR[:, t, 128 * p:128 * p + 128]) for t in range(NT)])
                        ins = mm_all(o[:, 129 * q + 128:129 * q + 129],
                                     [(kR[:, t, 128 * p:128 * p + 128], ones[0:R, 0:1]) for t in range(NT)])
                    ins.then_inc(tile_full, 1)
                pe.wait_ge(*made(L + ".ctxd"))
                pe.wait_ge(*evacd(L + ".ctx"))
                o = begin(L + ".den", 0)
                for t in range(NT):
                    ins = mm_all(o[0:R, 8 * t:8 * t + 8], [(qT[:, p, t * R:(t + 1) * R], ksd[:, p, :]) for p in range(4)])
                ins.then_inc(tile_full, 1)
                for t in range(NT):
                    o = begin(L + ".num", t)
                    for p in range(4):
                        ins = nc.tensor.matmul(o[0:R, 128 * p:128 * p + 128], qT[:, p, t * R:(t + 1) * R],
                                               ctxd[:, p, :], start=True, stop=True)
                    ins.then_inc(tile_full, 1)

            pe.wait_ge(*made("pre.consts"))
            hot = B(0, 2).bitcast(BF16)
            zero = B(2).bitcast(BF16)
            pe.wait_ge(*made("pre.ids"))
            for b in range(7):
                nc.tensor.matmul(PSF[0:R, 512 * b:512 * b + 512], zero[0:EP, 0:R], zero[0:EP, 0:512],
                                 start=True, stop=False, skip_group_check=True)

            def pieces():
                for s in range(NT):
                    a = 0
                    while a < N:
                        c = s * N + a
                        b = min(N, a + 512 - c % 512)
                        yield s, a, b, c
                        a = b
            with pe.Fori(0, ET // 2) as it:
                for u in range(2):
                    pe.wait_ge(l1_hot, it * 2 + (u + 1))
                    o_s = hot[0:EP, 2 * u * 1024:2 * u * 1024 + N]
                    o_d = hot[0:EP, (2 * u + 1) * 1024:(2 * u + 1) * 1024 + N]
                    for s, a, b, c in pieces():
                        ins = nc.tensor.matmul(PSF[0:R, c:c + b - a], o_s[:, s * R:(s + 1) * R], o_d[:, a:b],
                                               start=False, stop=False, skip_group_check=True)
                    ins.then_inc(l1_used, 1)
            pe.wait_ge(*made("pre.counts"))
            o = begin("pre.cnt", 0)
            for a, b in ((0, 512), (512, N)):
                ins = mm_all(o[0:R, a:b], [(ones[0:R, 0:R], AC[0:R, t, a:b]) for t in range(NT)])
            ins.then_inc(tile_full, 1)
            xnA, xnTA = xn, xnT
            turn_rows("L0.xnT", xnA, lambda t: pe.wait_ge(*made("L0.xn", t + 1)))
            pe.wait_ge(*made("pre.agg"))
            hR, hT, agT = rowsof(B(2)), colsof(B(3)), colsof(B(4))

            def conv(L, i, h, ht):
                aggregate(f"{L}.agg{i}", h)
                pe.wait_ge(*weight_ready(f"L0_gnn_Wl{i}"))
                pe.wait_ge(*weight_ready(f"L0_gnn_Wr{i}"))
                pe.wait_ge(*evacd(f"{L}.agg{i}"))
                dense_rows(f"{L}.conv{i}", [(agT, weight(f"L0_gnn_Wl{i}")), (ht, weight(f"L0_gnn_Wr{i}"))])

            def qkv(L):
                pe.wait_ge(*weight_ready(L + "_wq"))
                dense_cols(L + ".q", xnT, weight(L + "_wq"), KC)
                pe.wait_ge(*weight_ready(L + "_wk"))
                dense_rows(L + ".k", [(xnT, weight(L + "_wk"))])
                pe.wait_ge(*weight_ready(L + "_wv"))
                dense_rows(L + ".v", [(xnT, weight(L + "_wv"))])

            def att_out(L):
                turn_rows(L + ".oT", oR, lambda t: pe.wait_ge(*evacd(L + ".num", t)))
                pe.wait_ge(*evacd(L + ".oT"))
                pe.wait_ge(*weight_ready(L + "_wo"))
                dense_rows(L + ".out", [(oT, weight(L + "_wo"))])

            pe.wait_ge(*evacd("L0.xnT"))
            conv("L0", 0, xnA, xnTA)
            qkv("L0")
            turn_rows("L0.hT0", hR, lambda t: pe.wait_ge(*made("L0.h0", t + 1)))
            conv("L0", 1, hR, hT)
            pe.wait_ge(*made("L0.kfm"))
            pe.wait_ge(*made("L0.qfm"))
            pe.wait_ge(*evacd("L0.v"))
            attention("L0")
            turn_rows("L0.hT1", hR, lambda t: pe.wait_ge(*made("L0.h1", t + 1)))
            conv("L0", 2, hR, hT)
            att_out("L0")

            def router(stage, a, which, n):
                o = begin(stage, 0)
                for t in range(NT):
                    ins = mm_all(o[0:R, n * t:n * t + n], [(a[:, c, t * R:(t + 1) * R], wr[:, which, c, 0:n])
                                                          for c in range(KC)])
                ins.then_inc(tile_full, 1)

            def turn_probs(stage, a, n):
                o = begin(stage, 0)
                for t in range(NT):
                    ins = nc.tensor.transpose(o[0:n, 128 * t:128 * t + R], a[0:R, t, 0:n], ident[0:R, 0:R])
                ins.then_inc(tile_full, 1)

            def level(lv, n, a):
                fh, fhT = rowsof(B(2), 64 * n), colsof(B(3), n // 2)
                router(f"F{lv}.lg", a, lv, n)
                pe.wait_ge(*made(f"F{lv}.prob"))
                turn_probs(f"F{lv}.pT", sm[:, 0, :, :], n)
                pe.wait_ge(*weight_ready(f"L0_ffn_W1_{lv}"))
                dense_rows(f"F{lv}.h", [(a, weight(f"L0_ffn_W1_{lv}"))], w=64 * n)
                turn_rows(f"F{lv}.hT", fh, lambda t: pe.wait_ge(*made(f"F{lv}.hw", t + 1)), k=n // 2)
                pe.wait_ge(*evacd(f"F{lv}.hT"))
                pe.wait_ge(*evacd(f"F{lv}.pT"))
                pe.wait_ge(*weight_ready(f"L0_ffn_W2_{lv}"))
                dense_rows(f"F{lv}.y", [(fhT, weight(f"L0_ffn_W2_{lv}"))], k=n // 2,
                           extra=lambda t: [(combT[0:n, t * R:(t + 1) * R], eb[0:n, lv, :])])

            if last >= 2:
                turn_rows("L0f.xnT", xn, lambda t: pe.wait_ge(*made("L0f.xn", t + 1)))
                pe.wait_ge(*evacd("L0f.xnT"))
                pe.wait_ge(consts_in, 2 * 16)
                pe.wait_ge(*ebias_ready(2))
                level(0, 4, xnT)
                turn_rows("F1.xT", rowsof(B(4)), lambda t: pe.wait_ge(*evacd("F0.y", t)))
                pe.wait_ge(*evacd("F1.xT"))
                level(1, 8, colsof(B(5)))

            if last >= 3:
                turn_rows("L1.xnT", xn, lambda t: pe.wait_ge(*made("L1.xn", t + 1)))
                pe.wait_ge(*evacd("L1.xnT"))
                aggregate("L1.agg0", xn)
                pe.wait_ge(*weight_ready("L1_gnn_W_self1"))
                pe.wait_ge(*weight_ready("L1_gnn_W_neigh1"))
                pe.wait_ge(*evacd("L1.agg0"))
                dense_rows("L1.g0", [(xnT, weight("L1_gnn_W_self1")), (agT, weight("L1_gnn_W_neigh1"))])
                pe.wait_ge(*weight_ready("L1_mix_W_in"))
                xmT = colsof(B(6))
                dense_cols("L1.xm", xnT, weight("L1_mix_W_in"), KC)
                pe.wait_ge(*evacd("L1.xm"))
                pe.wait_ge(blocks_in, 8 * 16)
                for t in range(NT):
                    o = begin("L1.mq", t)
                    for c in range(KC):
                        ins = nc.tensor.matmul(o[0:R, 64 * c:64 * c + 64], xmT[:, c, t * R:(t + 1) * R], bdq[:, :],
                                               start=True, stop=True)
                    ins.then_inc(tile_full, 1)
                for g2 in range(2):
                    halves_stage("L1.mk", g2, lambda lo, hi: [(bdk[:, c, :], xmT[:, 2 * g2 + c, lo:hi]) for c in range(2)])
                for t in range(NT):
                    o = begin("L1.mv", t)
                    for c in range(KC):
                        ins = nc.tensor.matmul(o[0:R, 128 * c:128 * c + 128], xmT[:, c, t * R:(t + 1) * R], bdv[:, :],
                                               start=True, stop=True)
                    ins.then_inc(tile_full, 1)
                turn_rows("L1.hT", hR, lambda t: pe.wait_ge(*made("L1.h", t + 1)))
                pe.wait_ge(*evacd("L1.hT"))
                aggregate("L1.agg1", hR)
                pe.wait_ge(*weight_ready("L1_gnn_W_self2"))
                pe.wait_ge(*weight_ready("L1_gnn_W_neigh2"))
                pe.wait_ge(*evacd("L1.agg1"))
                dense_rows("L1.g1", [(hT, weight("L1_gnn_W_self2")), (agT, weight("L1_gnn_W_neigh2"))])
                mqR = rowsof(B(7), 256)
                mkT = colsof(B(8), 2)
                mkR = B(7)[0:R, 1280:2560].rearrange("p (t f) -> p t f", t=NT)
                mvR = rowsof(B(9))
                mqT = colsof(B(6), 2)
                turn_rows("L1.qT", mqR, lambda t: pe.wait_ge(*made("L1.qs", t + 1)), k=2)
                pe.wait_ge(*made("L1.ks"))
                for t in range(NT):
                    o = begin("L1.kR", t)
                    for g2 in range(2):
                        ins = nc.tensor.transpose(o[0:R, 128 * g2:128 * g2 + 128], mkT[:, g2, t * R:(t + 1) * R],
                                                  ident[:, :])
                    ins.then_inc(tile_full, 1)
                pe.wait_ge(*evacd("L1.kR"))
                pe.wait_ge(*evacd("L1.mv"))
                o = begin("L1.kv", 0)
                for g2 in range(2):
                    ins = mm_all(o[:, 256 * g2:256 * g2 + 256],
                                 [(mkR[:, t, 128 * g2:128 * g2 + 128], mvR[:, t, 256 * g2:256 * g2 + 256])
                                  for t in range(NT)])
                ins.then_inc(tile_full, 1)
                pe.wait_ge(*made("L1.kvd"))
                pe.wait_ge(*evacd("L1.kv"))
                pe.wait_ge(*evacd("L1.qT"))
                for t in range(NT):
                    o = begin("L1.num", t)
                    for g2 in range(2):
                        ins = nc.tensor.matmul(o[0:R, 256 * g2:256 * g2 + 256], mqT[:, g2, t * R:(t + 1) * R],
                                               kvd[:, g2, :], start=True, stop=True)
                    ins.then_inc(tile_full, 1)
                turn_rows("L1.oT", rowsof(B(8)), lambda t: pe.wait_ge(*evacd("L1.num", t)))
                pe.wait_ge(*evacd("L1.oT"))
                pe.wait_ge(*weight_ready("L1_mix_W_out"))
                dense_rows("L1.out", [(colsof(B(9)), weight("L1_mix_W_out"))])

            if last >= 4:
                turn_rows("L1f.xnT", xn, lambda t: pe.wait_ge(*made("L1f.xn", t + 1)))
                o = begin("sort.deg", 0)
                pe.wait_ge(*made("sort.srcdeg"))
                for t in range(NT):
                    ins = nc.tensor.matmul(o[0:R, 128 * t:128 * t + R], small[0:R, t:t + 1].to_broadcast([R, R]),
                                           ident[0:R, 0:R], start=True, stop=True)
                ins.then_inc(tile_full, 1)

                pe.wait_ge(*evacd("L1f.xnT"))
                for j, gname in enumerate("ifoc"):
                    pe.wait_ge(*weight_ready("L1_wx_" + gname))
                    dense_cols(f"L1f.gx{j}", lx, weight("L1_wx_" + gname), KC)
                pe.wait_ge(*evacd("L1f.gx3"))
                pe.wait_ge(*made("L1f.split"))
                pe.wait_ge(*made("sort.offs"))
                pe.wait_ge(*made("sort.consts"))
                pe.wait_ge(*evacd("sort.deg"))
                pe.sem_inc(rk_cum, 1)

                def step(t):
                    pe.wait_ge(ls_h, t * 3 + 3)
                    for c in range(KC):
                        for s in range(3):
                            for j in range(4):
                                ins = nc.tensor.matmul(ls_sum[32 * j:32 * j + 32, :], ls_parts[:, c, :],
                                                       ls_w[:, s, j, c, :], start=(c == 0 and s == 0),
                                                       stop=(c == KC - 1 and s == 2))
                    ins.then_inc(ls_full, 1)

                def fill(k):
                    for _ in range(k):
                        nc.tensor.matmul(PS[:, 3, 0:512], ls_w[:, 0, 0, 0, 0:128], ls_w[:, 0, 0, 0, :],
                                         start=True, stop=True)

                def rank(it, u):
                    pe.wait_ge(rk_hot, it * 2 + (u + 1))
                    pe.wait_ge(rk_seen, it * 2 + (u + 1))
                    pe.wait_ge(rk_pos, it * 2 + (u + 1))
                    for a, b in ((0, 512), (512, N)):
                        ins = mm_all(PS[0:EP, 1 + u, a:b], [(row0, offs_hi[:, a:b]), (row0, offs_lo[:, a:b]),
                                                            (oneb, seen[u][:, a:b]), (tri, hot_rank[u][:, a:b])])
                    ins.then_inc(rk_cum, 1)
                with pe.Fori(0, ET // 2) as it:
                    for u in range(2):
                        step(it * 2 + u)
                        rank(it, u)
                        fill(LS_FILL - 4)
                with pe.Fori(ET, N) as t:
                    step(t)
                    fill(LS_FILL)
                pe.wait_ge(ls_h, 3 * N + 3)
                for t in range(NT):
                    o = begin("L1f.hs", t)
                    for c in range(KC):
                        ins = nc.tensor.transpose(o[0:R, 128 * c:128 * c + 128], ls_out[:, c, t * R:(t + 1) * R],
                                                  ident[:, :])
                    ins.then_inc(tile_full, 1)

            if last >= 5:
                turn_rows("L2.xnT", xn, lambda t: pe.wait_ge(*made("L2.xn", t + 1)))
                pe.wait_ge(*evacd("L2.xnT"))
                for x in "qkv":
                    pe.wait_ge(*weight_ready("L2_gnn_W" + x))
                    dense_rows("L2.g" + x, [(xnT, weight("L2_gnn_W" + x))])
                qkv("L2")
                pe.wait_ge(*made("L2.kfm"))
                pe.wait_ge(*made("L2.qfm"))
                pe.wait_ge(*evacd("L2.v"))
                attention("L2")
                att_out("L2")
                pe.wait_ge(*made("L2.logit"))
                for j in range(20):
                    o = begin("L2.lT", j)
                    for q in range(4):
                        ins = nc.tensor.transpose(o[0:8, EP * q:EP * q + EP], logit[0:EP, 4 * j + q, :], ident[0:EP, 0:EP])
                    ins.then_inc(tile_full, 1)
                pe.wait_ge(*made("L2.flag"))
                for j in range(20):
                    o = begin("L2.fT", j)
                    for q in range(4):
                        ins = nc.tensor.transpose(o[0:8, EP * q:EP * q + EP],
                                                  flag[0:EP, 4 * j + q:4 * j + q + 1].to_broadcast([EP, 8]),
                                                  ident[0:EP, 0:EP])
                    ins.then_inc(tile_full, 1)
                pe.wait_ge(*made("L2.rowmax"))
                for j in range(2):
                    o = begin("L2.mR", j)
                    for q in range(40):
                        t = 40 * j + q
                        ins = nc.tensor.transpose(o[0:EP, 8 * q:8 * q + 8], lrow[:, t:E:ET], ident[0:8, 0:8])
                    ins.then_inc(tile_full, 1)
                pe.wait_ge(*evacd("L2.mR"))
                pe.wait_ge(*evacd("L2.out"))
                pe.wait_ge(*evacd("L2.oT"))
                for b in range(6):
                    nc.tensor.matmul(PSF[0:R, 512 * b:512 * b + 512], zero5[0:EP, 0:R], zero5[0:EP, 0:512],
                                     start=True, stop=False, skip_group_check=True)
                with pe.Fori(0, ET // 2) as it:
                    for u in range(2):
                        pe.wait_ge(pv_ready, it * 6 + (3 * u + 3))
                        for s in range(NT):
                            nc.tensor.matmul(PSF[0:R, 512 * s:512 * s + 512], hot_s[u][:, s * R:(s + 1) * R],
                                             pv[u][:, 0:512], start=False, stop=False, skip_group_check=True)
                            ins = nc.tensor.matmul(PSF[0:R, 2560 + 8 * s:2568 + 8 * s], hot_s[u][:, s * R:(s + 1) * R],
                                                   pv[u][:, 512:520], start=False, stop=False, skip_group_check=True)
                        ins.then_inc(pv_used, 1)
                pe.wait_ge(*made("L2.ysum"))
                turn_rows("L2.yT", rowsof(B(3)), lambda t: None)
                pe.wait_ge(*evacd("L2.yT"))
                pe.wait_ge(*weight_ready("L2_gnn_Wo"))
                dense_rows("L2.gout", [(colsof(B(4)), weight("L2_gnn_Wo"))])

            if last >= 6:
                turn_rows("L2f.xnT", xn, lambda t: pe.wait_ge(*made("L2f.xn", t + 1)))
                pe.wait_ge(*evacd("L2f.xnT"))
                router("L2f.lg", xnT, 2, 8)
                pe.wait_ge(*weight_ready("L2_ffn_sw1"))
                dense_cols("L2f.s1", xnT, weight("L2_ffn_sw1"), KC)
                pe.wait_ge(*made("L2f.prob"))
                turn_probs("L2f.cT", sm[:, 0, :, :], 8)
                pe.wait_ge(*evacd("L2f.s1"))
                pe.wait_ge(*evacd("L2f.cT"))
                pe.wait_ge(*ebias_ready(6))
                pe.wait_ge(*weight_ready("L2_ffn_sw2"))
                dense_rows("L2f.s2", [(colsof(B(2)), weight("L2_ffn_sw2"))],
                           extra=lambda t: [(combT[:, t * R:(t + 1) * R], eb[:, 0, :])])
                for j in range(2):
                    pe.wait_ge(*weight_ready(f"L2_w1_{j}"))
                    dense_cols(f"L2f.h{j}", xnT, weight(f"L2_w1_{j}"), KC)
                for j in range(2):
                    pe.wait_ge(*weight_ready(f"L2_w2_{j}"))
                    pe.wait_ge(*evacd(f"L2f.h{j}"))
                    for e in range(4):
                        for t in range(NT):
                            o = begin(f"L2f.eo{j}", 5 * e + t)
                            nc.tensor.matmul(o[0:R, 0:512], h1T[:, 4 * j + e, t * R:(t + 1) * R],
                                             weight(f"L2_w2_{j}")[:, e, :], start=True, stop=True).then_inc(tile_full, 1)

            if last >= 7:
                turn_rows("L3.xnT", xn, lambda t: pe.wait_ge(*made("L3.xn", t + 1)))
                pe.wait_ge(*evacd("L3.xnT"))
                pe.wait_ge(*weight_ready("L3_gnn_W1"))
                dense_cols("L3.x1", xnT, weight("L3_gnn_W1"), 2)
                pe.wait_ge(*weight_ready("L3_gnn_W2"))
                pe.wait_ge(*evacd("L3.x1"))
                dense_cols("L3.x2", colsof(B(2), 2), weight("L3_gnn_W2"), 4, k=2)
                pe.wait_ge(*weight_ready("L3_gnn_Wg"))
                pe.wait_ge(*evacd("L3.x2"))
                dense_rows("L3.xp", [(colsof(B(3)), weight("L3_gnn_Wg"))], w=256)
                pe.wait_ge(*made("L3.selfs"))
                for t in range(NT):
                    o = begin("L3.adjT", t)
                    for s in range(NT):
                        ins = nc.tensor.transpose(o[0:R, 128 * s:128 * s + R], AC[0:R, s, t * R:(t + 1) * R],
                                                  ident[0:R, 0:R])
                    ins.then_inc(tile_full, 1)

                def spread(stage, j, column):
                    o = begin(stage, j)
                    for t in range(NT):
                        ins = nc.tensor.matmul(o[0:R, 128 * t:128 * t + R], column(t).to_broadcast([R, R]),
                                               ident[0:R, 0:R], start=True, stop=True)
                    ins.then_inc(tile_full, 1)

                pe.wait_ge(*made("L3.sd"))
                for j in range(4):
                    spread("L3.sdB", j, lambda t: sd[0:R, j, t:t + 1])
                pe.wait_ge(*made("L3.mx"))
                for j in range(2):
                    spread("L3.mxB", j, lambda t: mxc[0:R, j, t:t + 1])
                pe.wait_ge(*made("L3.pt"))
                pe.wait_ge(*made("L3.onec"))
                pe.wait_ge(*evacd("L3.xp"))
                for t in range(NT):
                    o = begin("L3.gat", t)
                    for h in range(2):
                        ins = mm_all(o[0:R, 129 * h:129 * h + 129],
                                     [(pT[:, 5 * h + s, t * R:(t + 1) * R], xp[:, s, h, :]) for s in range(NT)])
                    ins.then_inc(tile_full, 1)
                turn_rows("L3.gT", og, lambda t: pe.wait_ge(*made("L3.og", t + 1)), k=2)
                pe.wait_ge(*weight_ready("L3_gnn_W3"))
                pe.wait_ge(*evacd("L3.gT"))
                dense_rows("L3.gout", [(colsof(B(3), 2), weight("L3_gnn_W3"))], k=2)
                qkv("L3")
                pe.wait_ge(*made("L3.kfm"))
                pe.wait_ge(*made("L3.qfm"))
                pe.wait_ge(*evacd("L3.v"))
                attention("L3")
                att_out("L3")

            if last >= 8:
                turn_rows("L3f.xnT", xn, lambda t: pe.wait_ge(*made("L3f.xn", t + 1)))
                pe.wait_ge(*evacd("L3f.xnT"))
                router("L3f.lg", xnT, 3, 8)
                pe.wait_ge(*made("L3f.prob"))
                turn_probs("L3f.cT", sm[:, 0, :, :], 8)
                pe.wait_ge(*evacd("L3f.cT"))
                pe.wait_ge(*ebias_ready(8))
                rows_stage("L3f.b", lambda t: [(combT[:, t * R:(t + 1) * R], eb[:, 0, :])])
                for e in range(9):
                    if e < 8:
                        for x, wname in (("i", f"L3_wi{e}"), ("g", f"L3_wg{e}"), ("o", f"L3_wo_{e}")):
                            pe.wait_ge(*weight_ready(wname))
                            dense_cols(f"L3f.{x}{e}", xnT, weight(wname), KC)
                    if e:
                        pe.wait_ge(*weight_ready(f"L3_wout{e - 1}"))
                        pe.wait_ge(*made(f"L3f.hid{e - 1}"))
                        dense_rows(f"L3f.y{e - 1}", [(colsof(B(5 + (e - 1) % 2)), weight(f"L3_wout{e - 1}"))])

        @block.scalar
        def _(act):
            st = Steps(act, act_step)

            def copy_rows(stage, dst, w=D, n=NT):
                for t in range(n):
                    act.wait_ge(*full(stage, t))
                    took(nc.scalar.activation(dst(t), bank(stage, t)[0:R, 0:w], ACT.Copy), stage, t)

            def copy_turned(stage, dst, k=KC):
                for t in range(NT):
                    act.wait_ge(*full(stage, t))
                    took(nc.scalar.activation(dst[:, :, t * R:(t + 1) * R],
                                              bank(stage, t)[:, 0:k * R].rearrange("p (c n) -> p c n", c=k),
                                              ACT.Copy), stage, t)

            def copy_cols(stage, dst, n, func=ACT.Copy, scale=1.0, bias=None):
                for c in range(n):
                    act.wait_ge(*full(stage, c))
                    kw = {"bias": bias(c)} if bias else {}
                    took(nc.scalar.activation(dst(c), slot(stage, c)[:, 0:N], func, scale=scale, **kw), stage, c)

            def exps(L):
                tq, tk = colsof(tmpB), rowsof(tmpB)
                for c in range(KC):
                    act.wait_ge(*made(L + ".qmin", c + 1))
                    make(nc.scalar.activation(tq[:, c, :], tq[:, c, :], ACT.Exp), L + ".qexp")
                for t in range(NT):
                    act.wait_ge(*made(L + ".kmin", t + 1))
                    make(nc.scalar.activation(tk[:, t, :], tk[:, t, :], ACT.Exp), L + ".kexp")

            hT, agT = colsof(B(3)), colsof(B(4))
            copy_turned("L0.xnT", xnT)
            copy_cols("L0.agg0", lambda c: agT[:, c, :], KC)
            copy_cols("L0.q", lambda c: qT[:, c, :], KC, scale=0.125)
            copy_rows("L0.k", lambda t: kR[:, t, :])
            copy_rows("L0.v", lambda t: vR[:, t, :])
            exps("L0")
            copy_turned("L0.hT0", hT)
            copy_cols("L0.agg1", lambda c: agT[:, c, :], KC)
            copy_turned("L0.hT1", hT)
            copy_cols("L0.agg2", lambda c: agT[:, c, :], KC)
            copy_turned("L0.oT", oT)

            def copy_probs(stage, n):
                act.wait_ge(*full(stage, 0))
                took(nc.scalar.activation(combT[0:n, :].rearrange("e (t p) -> e t p", t=NT),
                                          slot(stage, 0)[0:n, 0:640].rearrange("e (t p) -> e t p", t=NT)[:, :, 0:R],
                                          ACT.Copy), stage, 0)

            def exp_small(L, n):
                act.wait_ge(*made(L + ".sub"))
                make(nc.scalar.activation(sm[0:R, 1, :, 0:n], sm[0:R, 1, :, 0:n], ACT.Exp), L + ".pexp")

            if last >= 2:
                copy_turned("L0f.xnT", xnT)
                exp_small("F0", 4)
                copy_probs("F0.pT", 4)
                copy_turned("F0.hT", colsof(B(3), 2), 2)
                copy_rows("F0.y", lambda t: rowsof(B(4))[:, t, :])
                copy_turned("F1.xT", colsof(B(5)))
                exp_small("F1", 8)
                copy_probs("F1.pT", 8)
                copy_turned("F1.hT", colsof(B(3), 4), 4)
            if last >= 3:
                copy_turned("L1.xnT", xnT)
                copy_cols("L1.agg0", lambda c: agT[:, c, :], KC)
                act.wait_ge(consts_in, 2 * 16)
                cb = COL_AT["L1_mix_b_in"]
                copy_cols("L1.xm", lambda c: colsof(B(6))[:, c, :], KC, ACT.Identity,
                          bias=lambda c: cols[:, cb + c:cb + c + 1])
                mqR, mkT = rowsof(B(7), 256), colsof(B(8), 2)
                mkR = B(7)[0:R, 1280:2560].rearrange("p (t f) -> p t f", t=NT)
                for t in range(NT):
                    act.wait_ge(*evacd("L1.mq", t))
                    make(nc.scalar.activation(mqR[:, t, :], mqR[:, t, :], ACT.Exp), "L1.pexp")
                copy_cols("L1.mk", lambda c: mkT[:, c, :], 2)
                copy_rows("L1.mv", lambda t: rowsof(B(9))[:, t, :])
                act.wait_ge(*made("L1.kneg"))
                for c in range(2):
                    make(nc.scalar.activation(mkT[:, c, :], mkT[:, c, :], ACT.Exp, bias=small[:, 12 + c:13 + c],
                                              accum_out=small[:, 14 + c:15 + c]), "L1.kexps")
                copy_turned("L1.hT", hT)
                copy_cols("L1.agg1", lambda c: agT[:, c, :], KC)
                copy_turned("L1.qT", colsof(B(6), 2), 2)
                copy_rows("L1.kR", lambda t: mkR[:, t, :], 256)
                copy_rows("L1.num", lambda t: rowsof(B(8))[:, t, :])
                copy_turned("L1.oT", colsof(B(9)))
            if last >= 4:
                copy_turned("L1f.xnT", lx)
                act.wait_ge(*made("L1f.halfbias"))
                for j, gname in enumerate("ifoc"):
                    cb = COL_AT["L1_ffn_b_" + gname]
                    copy_cols(f"L1f.gx{j}", lambda c: ls_gx[:, 4 * j + c, :], KC, ACT.Identity,
                              scale=1.0 if gname == "c" else 0.5, bias=lambda c: cols[:, cb + c:cb + c + 1])
                with act.Fori(0, N) as t:
                    act.wait_ge(ls_pre, t + 1)
                    nc.scalar.activation(ls_gate[:, 0:16], ls_act[:, :], ACT.Tanh).then_inc(ls_sig, 1)
                    act.wait_ge(ls_cell, t * 2 + 2)
                    nc.scalar.activation(ls_th[:, :], ls_2c[:, :], ACT.Tanh, scale=0.5).then_inc(ls_tanh, 1)

            if last >= 5:
                copy_turned("L2.xnT", xnT)
                copy_cols("L2.q", lambda c: qT[:, c, :], KC)
                copy_rows("L2.k", lambda t: kR[:, t, :])
                copy_rows("L2.v", lambda t: vR[:, t, :])
                exps("L2")
                copy_turned("L2.oT", oT)
                act.wait_ge(*evacd("L2.out"))
                for j in range(20):
                    act.wait_ge(*full("L2.lT", j))
                    took(nc.scalar.activation(lrow.rearrange("h (p t) -> h t p", t=ET)[:, 4 * j:4 * j + 4, :],
                                              bank("L2.lT", j)[0:8, 0:500].rearrange("h (q p) -> h q p", q=4),
                                              ACT.Copy), "L2.lT", j)
                act.wait_ge(*evacd("L2.mR"))
                make(nc.scalar.activation(logit[0:EP, :, :], logit[0:EP, :, :], ACT.Exp), "L2.pexp")
                copy_turned("L2.yT", colsof(B(4)))

            def col(name, c):
                return cols[:, COL_AT[name] + c:COL_AT[name] + c + 1]

            if last >= 6:
                copy_turned("L2f.xnT", xnT)
                copy_cols("L2f.s1", lambda c: colsof(B(2))[:, c, :], KC, ACT.Relu, bias=lambda c: col("L2_ffn_sb1", c))
                exp_small("L2f", 8)
                copy_probs("L2f.cT", 8)
                for j in range(2):
                    copy_cols(f"L2f.h{j}", lambda c: h1T[:, 4 * j + c, :], KC, ACT.Relu,
                              bias=lambda c: col("L2_ffn_b1", 4 * j + c))
            if last >= 7:
                copy_turned("L3.xnT", xnT)
                copy_cols("L3.x1", lambda c: colsof(B(2), 2)[:, c, :], 2, ACT.Relu, bias=lambda c: col("L3_gnn_b1", c))
                copy_cols("L3.x2", lambda c: colsof(B(3))[:, c, :], 4, ACT.Relu, bias=lambda c: col("L3_gnn_b2", c))
                for t in range(NT):
                    act.wait_ge(*full("L3.xp", t))
                    took(nc.scalar.activation(xp[:, t, :, 0:128], bank("L3.xp", t)[0:R, 0:256].rearrange(
                        "p (h f) -> p h f", h=2), ACT.Copy), "L3.xp", t)

                def copy_spread(stage, n, dst):
                    for j in range(n):
                        act.wait_ge(*full(stage, j))
                        took(nc.scalar.activation(dst(j).rearrange("p (t n) -> p t n", t=NT),
                                                  slot(stage, j)[0:R, 0:640].rearrange("p (t n) -> p t n", t=NT)[:, :, 0:R],
                                                  ACT.Copy), stage, j)
                copy_spread("L3.sdB", 4, lambda j: sB[:, j, :])
                copy_spread("L3.mxB", 2, lambda j: mB[:, j, :])
                for j in range(10):
                    act.wait_ge(*made("L3.sub", j + 1))
                    make(nc.scalar.activation(pT[:, j, :], pT[:, j, :], ACT.Exp), "L3.pexp")
                copy_turned("L3.gT", colsof(B(3), 2), 2)
                copy_cols("L3.q", lambda c: qT[:, c, :], KC, ACT.Identity, bias=lambda c: col("L3_mix_bq", c))
                exps("L3")
                copy_turned("L3.oT", oT)
            if last >= 8:
                copy_turned("L3f.xnT", xnT)
                exp_small("L3f", 8)
                copy_probs("L3f.cT", 8)
                for e in range(8):
                    if e:
                        act.wait_ge(*made(f"L3f.hid{e - 1}"))
                    for b, x, at, func in ((2, "i", 0, ACT.Sigmoid), (3, "g", 8, ACT.Tanh), (4, "o", 12, ACT.Sigmoid)):
                        copy_cols(f"L3f.{x}{e}", lambda c: colsof(B(b))[:, c, :], KC, func,
                                  bias=lambda c: col("L3_ffn_b", 16 * e + at + c))
                    act.wait_ge(*made(f"L3f.cell{e}"))
                    make(nc.scalar.activation(colsof(B(2)), colsof(B(2)), ACT.Tanh), f"L3f.tc{e}")

        @block.vector
        def _(dve):
            st = Steps(dve, dve_step)
            V = nc.vector

            def row(name, w=D):
                for names in ROWS.values():
                    if name in names:
                        return rows[0:R, names.index(name), 0:w]

            def rsqrt():
                v, y, p = nw[0:R, 0, :], nw[0:R, 1, :], nw[0:R, 2, :]
                st.done(V.tensor_scalar(nwi[0:R, :], v.bitcast(I32), 1, None, ALU.logical_shift_right))
                st.after()
                st.done(V.tensor_scalar(nwi[0:R, :], nwi[0:R, :], -1.0, float(0x5F3759DF), ALU.mult, ALU.add))
                st.after()
                y0 = nwi[0:R, :].bitcast(F32)
                for k in range(4):
                    a = y0 if k == 0 else y
                    st.done(V.tensor_tensor(p, a, a, ALU.mult))
                    st.after()
                    st.done(V.scalar_tensor_tensor(p, p, -0.5, v, ALU.mult, ALU.mult))
                    st.after()
                    st.done(V.scalar_tensor_tensor(y, p, 1.5, a, ALU.add, ALU.mult))
                    st.after()
                return y

            def normalize(src, put):
                for t in range(NT):
                    st.done(V.bn_stats(stats[0:R, t, :], src[:, t, :]))
                st.after()
                for t in range(NT):
                    st.done(V.bn_aggr(mv[0:R, t, :], stats[0:R, t, :]))
                st.after()
                st.done(V.tensor_scalar(nw[0:R, 0, :], mv[0:R, :, 1], 1e-5, None, ALU.add))
                st.after()
                y = rsqrt()
                for t in range(NT):
                    put(t, mv[0:R, t, 0:1], y[:, t:t + 1])

            Xr = X[0:R, :, :]

            def norm_x(stage, dst=None):
                d = xn if dst is None else dst
                normalize(Xr, lambda t, m, r: make(V.tensor_scalar(d[:, t, :], Xr[:, t, :], m, r, ALU.subtract, ALU.mult),
                                                   stage + ".xn"))

            dve.wait_ge(edges_in, 16)
            st.done(V.memset(B(2).bitcast(BF16)[:, 0:1024], 0.0))
            make(V.tensor_copy(ids[0:EP, :, :], src_i[0:EP, :, :]), "pre.ids")
            dve.wait_ge(*made("pre.ids"))
            dve.wait_ge(*made("pre.consts"))
            st.after()
            hot = B(0, 2).bitcast(BF16)

            def one_hot(it, u):
                V.tensor_scalar(hot[0:EP, 2 * u * 1024:2 * u * 1024 + N], iota[0:EP, :],
                                ids[0:EP, 0, bass.ds(it * 2 + u, 1)], None, ALU.is_equal)
                V.tensor_scalar(hot[0:EP, (2 * u + 1) * 1024:(2 * u + 1) * 1024 + N], iota[0:EP, :],
                                ids[0:EP, 1, bass.ds(it * 2 + u, 1)], None, ALU.is_equal).then_inc(l1_hot, 1)
            for u in range(2):
                one_hot(0, u)
            with dve.Fori(1, ET // 2) as it:
                for u in range(2):
                    dve.wait_ge(l1_used, it * 2 + (u - 1))
                    one_hot(it, u)
            dve.wait_ge(l1_used, ET)
            for t in range(NT):
                make(V.tensor_copy(AC[0:R, t, :], PSF[0:R, t * N:(t + 1) * N]), "pre.counts")
            dve.wait_ge(*made("pre.counts"))
            dve.wait_ge(*full("pre.cnt", 0))
            rc = B(3)[0:R, 0:N]
            took(V.tensor_scalar(rc, slot("pre.cnt", 0)[0:R, 0:N], 1.0, None, ALU.max), "pre.cnt", 0)
            dve.wait_ge(*evacd("pre.cnt"))
            st.done(V.reciprocal(rc, rc))
            st.after()
            for t in range(NT):
                make(V.tensor_tensor(AH[0:R, t, :], AC[0:R, t, :], rc, ALU.mult), "pre.agg")
            dve.wait_ge(x_in, 16)
            norm_x("L0")
            hR, u5 = rowsof(B(2)), lnbuf
            dve.wait_ge(*rows_ready(1))
            dve.wait_ge(consts_in, 2 * 16)

            def feature_maps(L):
                tq, tk = colsof(tmpB), rowsof(tmpB)
                for c in range(KC):
                    dve.wait_ge(*made(L + ".qexp", c + 1))
                    make(V.scalar_tensor_tensor(qT[:, c, :], qT[:, c, :], 0.0, tq[:, c, :], ALU.max, ALU.add), L + ".qfm")
                for t in range(NT):
                    dve.wait_ge(*made(L + ".kexp", t + 1))
                    make(V.scalar_tensor_tensor(kR[:, t, :], kR[:, t, :], 0.0, tk[:, t, :], ALU.max, ALU.add), L + ".kfm")

            def conv(i):
                stage = f"L0.conv{i}"
                for t in range(NT):
                    dve.wait_ge(*full(stage, t))
                    took(V.tensor_tensor(u5[:, t, :], bank(stage, t)[0:R, :], row(f"L0_gnn_bl{i}"), ALU.add), stage, t)
                if i:
                    dve.wait_ge(*evacd(stage))
                    dve.wait_ge(*made(f"L0.h{i - 1}"))
                    for t in range(NT):
                        st.done(V.tensor_tensor(u5[:, t, :], u5[:, t, :], hR[:, t, :], ALU.add))
                    st.after()
                dve.wait_ge(*evacd(stage))

                def put(t, m, r):
                    st.done(V.tensor_scalar(u5[:, t, :], u5[:, t, :], m, r, ALU.subtract, ALU.mult))
                normalize(u5, put)
                st.after()
                for t in range(NT):
                    st.done(V.tensor_tensor(u5[:, t, :], u5[:, t, :], row(f"L0_gnn_g{i}"), ALU.mult))
                st.after()
                for t in range(NT):
                    st.done(V.tensor_tensor(u5[:, t, :], u5[:, t, :], row(f"L0_gnn_b{i}"), ALU.add))
                st.after()
                slope = cols[0:R, COL_AT["a_prelu"]:COL_AT["a_prelu"] + 1]
                for t in range(NT):
                    st.done(V.tensor_scalar(hR[:, t, :], u5[:, t, :], 0.0, slope, ALU.min, ALU.mult))
                st.after()
                for t in range(NT):
                    ins = V.scalar_tensor_tensor(hR[:, t, :], u5[:, t, :], 0.0, hR[:, t, :], ALU.max, ALU.add)
                    if i < 2:
                        make(ins, f"L0.h{i}")
                    else:
                        st.done(ins)
                if i == 2:
                    st.after()
                    for t in range(NT):
                        st.done(V.tensor_tensor(Xr[:, t, :], Xr[:, t, :], hR[:, t, :], ALU.add))
                    st.after()

            def attention(L, eps_op, eps):
                for j in range(2):
                    dve.wait_ge(*full(L + ".ctx", j))
                    o = bank(L + ".ctx", j)
                    for q in range(2):
                        p = 2 * j + q
                        for h in range(2):
                            a = 64 * h
                            make(V.tensor_copy(ksd[a:a + 64, p, 2 * p + h:2 * p + h + 1],
                                               o[a:a + 64, 129 * q + 128:129 * q + 129]), L + ".ctxd")
                            ins = V.tensor_copy(ctxd[a:a + 64, p, a:a + 64], o[a:a + 64, 129 * q + a:129 * q + a + 64])
                            if (q, h) == (1, 1):
                                took(ins, L + ".ctx", j)
                            else:
                                st.done(ins)
                dve.wait_ge(*full(L + ".den", 0))
                took(V.tensor_scalar(den[0:R, :, :], bank(L + ".den", 0)[0:R, 0:40].rearrange("p (t h) -> p t h", t=NT),
                                     eps, None, eps_op), L + ".den", 0)
                dve.wait_ge(*evacd(L + ".den"))
                st.done(V.reciprocal(den[0:R, :, :], den[0:R, :, :]))
                st.after()
                for t in range(NT):
                    dve.wait_ge(*full(L + ".num", t))
                    took(V.tensor_tensor(oR[:, t, :].rearrange("p (h d) -> p h d", h=H),
                                         bank(L + ".num", t)[0:R, :].rearrange("p (h d) -> p h d", h=H),
                                         den[0:R, t, :].unsqueeze(2).to_broadcast([R, H, 64]), ALU.mult), L + ".num", t)

            def add_out(stage, bias, done):
                for t in range(NT):
                    dve.wait_ge(*full(stage, t))
                    took(V.tensor_tensor(u5[:, t, :], bank(stage, t)[0:R, :], bias, ALU.add), stage, t)
                    dve.wait_ge(*evacd(stage, t))
                    ins = V.tensor_tensor(Xr[:, t, :], Xr[:, t, :], u5[:, t, :], ALU.add)
                    if done:
                        make(ins, done)
                    else:
                        st.done(ins)
                if done:
                    dve.wait_ge(*made(done))
                else:
                    st.after()

            conv(0)
            feature_maps("L0")
            conv(1)
            attention("L0", ALU.add, 1e-8)
            conv(2)
            add_out("L0.out", row("L0_mix_b_out"), "L0.done")

            def bc(ap, n):
                return ap.unsqueeze(2).to_broadcast([R, NT, n])

            def pick2(v, n):
                rv = rev8[0:R, 0:n].unsqueeze(1).to_broadcast([R, NT, n])
                s, w, hot1 = sm[0:R, 3, :, 0:n], sm[0:R, 4, :, 0:n], sm[0:R, 2, :, 0:n]
                m = smr[0:R, 0, :, 0]
                cur = v
                for k in range(2):
                    st.done(V.reduce_max(m, cur, AX_X))
                    st.after()
                    st.done(V.tensor_tensor(s, cur, bc(m, n), ALU.is_equal))
                    st.after()
                    st.done(V.tensor_tensor(s, s, rv, ALU.mult))
                    st.after()
                    st.done(V.reduce_max(m, s, AX_X))
                    st.after()
                    o = hot1 if k == 0 else sm[0:R, 5, :, 0:n]
                    st.done(V.tensor_tensor(o, s, bc(m, n), ALU.is_equal))
                    st.after()
                    if k == 0:
                        st.done(V.scalar_tensor_tensor(w, o, -BIG, cur, ALU.mult, ALU.add))
                        st.after()
                        cur = w
                st.done(V.tensor_tensor(hot1, hot1, sm[0:R, 5, :, 0:n], ALU.add))
                st.after()
                return hot1

            def softmax_small(L, lg_stage, n, bias=None):
                lg = sm[0:R, 6, :, 0:n]
                dve.wait_ge(*full(lg_stage, 0))
                o = bank(lg_stage, 0)[0:R, 0:NT * n].rearrange("p (t e) -> p t e", t=NT)
                if bias is None:
                    took(V.tensor_copy(lg, o), lg_stage, 0)
                else:
                    took(V.tensor_tensor(lg, o, bias, ALU.add), lg_stage, 0)
                dve.wait_ge(*evacd(lg_stage))
                st.done(V.reduce_max(smr[0:R, 1, :, 0], lg, AX_X))
                st.after()
                make(V.tensor_tensor(sm[0:R, 1, :, 0:n], lg, bc(smr[0:R, 1, :, 0], n), ALU.subtract), L + ".sub")
                dve.wait_ge(*made(L + ".pexp"))
                return lg

            def over_sum(L, dst, src, n, tiny=0.0):
                st.done(V.reduce_sum(smr[0:R, 2, :, 0], src, AX_X))
                st.after()
                if tiny:
                    st.done(V.tensor_scalar(smr[0:R, 2, :, 0], smr[0:R, 2, :, 0], tiny, None, ALU.add))
                    st.after()
                st.done(V.reciprocal(smr[0:R, 3, :, 0], smr[0:R, 2, :, 0]))
                st.after()
                make(V.tensor_tensor(dst, src, bc(smr[0:R, 3, :, 0], n), ALU.mult), L + ".prob") if L else \
                    st.done(V.tensor_tensor(dst, src, bc(smr[0:R, 3, :, 0], n), ALU.mult))

            def level(lv, n):
                L = f"F{lv}"
                softmax_small(L, L + ".lg", n)
                p = sm[0:R, 0, :, 0:n]
                over_sum(L, p, sm[0:R, 1, :, 0:n], n)
                dve.wait_ge(*made(L + ".prob"))
                hot2 = pick2(p, n)
                fh = rowsof(B(2), 64 * n)
                for t in range(NT):
                    dve.wait_ge(*full(L + ".h", t))
                    v = fh[:, t, :].rearrange("p (e f) -> p e f", e=n)
                    took(V.tensor_tensor(v, bank(L + ".h", t)[0:R, 0:64 * n].rearrange("p (e f) -> p e f", e=n),
                                         hot2[:, t, :].unsqueeze(2).to_broadcast([R, n, 64]), ALU.mult), L + ".h", t)
                    dve.wait_ge(*evacd(L + ".h", t))
                    st.done(V.tensor_tensor(fh[:, t, :], fh[:, t, :], row(f"L0_ffn_b1_{lv}", 64 * n), ALU.add))
                    st.after()
                    make(V.scalar_tensor_tensor(v, v, 0.0, p[:, t, :].unsqueeze(2).to_broadcast([R, n, 64]),
                                                ALU.max, ALU.mult), L + ".hw")

            if last >= 2:
                norm_x("L0f")
                dve.wait_ge(*rows_ready(2))
                level(0, 4)
                level(1, 8)
                for t in range(NT):
                    dve.wait_ge(*full("F1.y", t))
                    took(V.tensor_tensor(Xr[:, t, :], bank("F1.y", t)[0:R, :], Xr[:, t, :], ALU.add), "F1.y", t)
                dve.wait_ge(*evacd("F1.y"))

            if last >= 3:
                norm_x("L1")
                dve.wait_ge(*rows_ready(3))
                for t in range(NT):
                    dve.wait_ge(*full("L1.g0", t))
                    took(V.tensor_tensor(u5[:, t, :], bank("L1.g0", t)[0:R, :], row("L1_gnn_b1"), ALU.add), "L1.g0", t)
                    dve.wait_ge(*evacd("L1.g0", t))
                    make(V.tensor_scalar(hR[:, t, :], u5[:, t, :], 0.0, None, ALU.max), "L1.h")
                mq4 = rowsof(B(7), 256).rearrange("p t (h s) -> p t h s", h=H)
                for t in range(NT):
                    dve.wait_ge(*full("L1.mq", t))
                    o = bank("L1.mq", t)[0:R, 0:256].rearrange("p (h s) -> p h s", h=H)
                    st.done(V.reduce_max(den[0:R, t, :], o, AX_X))
                    st.after()
                    took(V.tensor_tensor(mq4[:, t], o, den[0:R, t, :].unsqueeze(2).to_broadcast([R, H, 32]),
                                         ALU.subtract), "L1.mq", t)
                for t in range(NT):
                    dve.wait_ge(*made("L1.pexp", t + 1))
                    st.done(V.reduce_sum(den[0:R, t, :], mq4[:, t], AX_X))
                    st.after()
                    st.done(V.reciprocal(den[0:R, t, :], den[0:R, t, :]))
                    st.after()
                    make(V.tensor_tensor(mq4[:, t], mq4[:, t], den[0:R, t, :].unsqueeze(2).to_broadcast([R, H, 32]),
                                         ALU.mult), "L1.qs")
                mkT = colsof(B(8), 2)
                dve.wait_ge(*evacd("L1.mk"))
                make(V.reduce_max(small[:, 12:14], mkT, AX_X, negate=True), "L1.kneg")
                dve.wait_ge(*made("L1.kexps"))
                st.done(V.reciprocal(small[:, 16:18], small[:, 14:16]))
                st.after()
                for c in range(2):
                    make(V.tensor_scalar(mkT[:, c, :], mkT[:, c, :], small[:, 16 + c:17 + c], None, ALU.mult), "L1.ks")
                for t in range(NT):
                    dve.wait_ge(*full("L1.g1", t))
                    took(V.tensor_tensor(u5[:, t, :], bank("L1.g1", t)[0:R, :], row("L1_gnn_b2"), ALU.add), "L1.g1", t)
                    dve.wait_ge(*evacd("L1.g1", t))
                    st.done(V.scalar_tensor_tensor(Xr[:, t, :], u5[:, t, :], 0.0, Xr[:, t, :], ALU.max, ALU.add))
                st.after()
                dve.wait_ge(*full("L1.kv", 0))
                for j in range(4):
                    a = 32 * j
                    ins = V.tensor_copy(kvd[a:a + 32, :, 64 * j:64 * j + 64],
                                        bank("L1.kv", 0)[a:a + 32, :].rearrange("p (g n) -> p g n", g=2)[
                                            :, :, 64 * j:64 * j + 64])
                    if j < 3:
                        make(ins, "L1.kvd")
                    else:
                        took(ins, "L1.kv", 0)
                add_out("L1.out", row("L1_mix_b_out"), "L1.done")

            if last >= 4:
                make(V.reduce_sum(small[0:R, 0:5], AC[0:R, :, :], AX_X), "sort.srcdeg")
                fio = COL_AT["L1_ffn_b_f"]
                make(V.tensor_scalar(cols[:, fio:fio + 12], cols[:, fio:fio + 12], 0.5, None, ALU.mult), "L1f.halfbias")
                norm_x("L1f")
                for j, gname in enumerate("ifoc"):
                    w = weight("L1_wh_" + gname)
                    dve.wait_ge(*weight_ready("L1_wh_" + gname))
                    st.done(V.tensor_scalar(w, w, 0.5 if gname == "c" else 0.25, None, ALU.mult))
                    st.after()
                    quarter = [w[:, :, :].rearrange("p k (c q n) -> p k c q n", c=KC, q=4)[:, :, :, q] for q in range(4)]
                    part = [[ls_w[:, s, q, :, 128 * j:128 * j + 128].rearrange("p k (c n) -> p k c n", c=KC)
                             for q in range(4)] for s in range(3)]
                    for s in range(3):
                        for q in range(4):
                            ins = V.tensor_copy(part[s][q], quarter[q])
                            if s == 2 and q == 3:
                                make(ins, "L1f.split")
                            else:
                                st.done(ins)
                        st.after()
                        if s < 2:
                            for q in range(4):
                                st.done(V.tensor_tensor(quarter[q], quarter[q], part[s][q], ALU.subtract))
                            st.after()
                V.memset(ls_gate[:, 16:20], 0.0).then_inc(ls_cell, 1)
                V.memset(ls_parts[:, :, :], 0.0).then_inc(ls_h, 3)
                dve.wait_ge(*full("sort.deg", 0))
                took(V.tensor_copy(cnt_src.rearrange("p (t n) -> p t n", t=NT),
                                   slot("sort.deg", 0)[0:R, 0:640].rearrange("p (t n) -> p t n", t=NT)[:, :, 0:R]), "sort.deg", 0)

                dve.wait_ge(*evacd("sort.deg"))
                st.done(V.memset(zeros, 0.0))
                st.after()
                st.done(V.tensor_tensor_scan(offs, zeros, cnt_src, 0.0, ALU.add, ALU.add))
                st.after()
                st.done(V.tensor_tensor(offs, offs, cnt_src, ALU.subtract))
                st.after()
                st.done(V.tensor_copy(offs_i, offs))
                st.after()
                st.done(V.tensor_scalar(offs_i, offs_i, 8, 8, ALU.logical_shift_right, ALU.logical_shift_left))
                st.after()
                st.done(V.tensor_copy(offs_hi, offs_i))
                st.after()
                make(V.tensor_tensor(offs_lo, offs, offs_hi, ALU.subtract), "sort.offs")
                V.memset(place_f[0:EP, 0:1], 0.0).then_inc(rk_pos, 2)

                def rank_hot(it, u):
                    V.tensor_scalar(hot_rank[u], iota[0:EP, :], ids[0:EP, 0, bass.ds(it * 2 + u, 1)], None,
                                    ALU.is_equal).then_inc(rk_hot, 1)

                def rank_place(it, u):
                    dve.wait_ge(rk_hot, it * 2 + (u + 1))
                    dve.wait_ge(rk_cum, it * 2 + (u + 2))
                    dve.wait_ge(rk_pos, it * 2 + (u + 2))
                    V.tensor_tensor_reduce(out=junk[u], in0=hot_rank[u], in1=PS[0:EP, 1 + u, 0:N], scale=1.0, scalar=0.0,
                                           op0=ALU.mult, op1=ALU.add, accum_out=small[0:EP, 42 + u:43 + u]).then_inc(rk_pos, 1)
                    dve.wait_ge(rk_pos, it * 2 + (u + 3))
                    V.tensor_copy(place_f[0:EP, bass.ds(it * 2 + u, 1)], small[0:EP, 42 + u:43 + u]).then_inc(rk_put, 1)

                def step(t):
                    dve.wait_ge(ls_full, t + 1)
                    V.transpose(ls_turn, ls_sum).then_inc(ls_part, 1)
                    dve.wait_ge(ls_part, t * 6 + 1)
                    V.reduce_sum(ls_act[:, :], ls_turn.rearrange("p (g s) -> p g s", s=32)[:, :, 0:3],
                                 AX_X).then_inc(ls_part, 1)
                    dve.wait_ge(ls_part, t * 6 + 2)
                    V.tensor_tensor(ls_act[:, :], ls_act[:, :], ls_gx[:, :, bass.ds(t, 1)].rearrange("p g o -> p (g o)"),
                                    ALU.add).then_inc(ls_pre, 1)
                    dve.wait_ge(ls_cell, t * 2 + 1)
                    dve.wait_ge(ls_sig, t + 1)
                    V.scalar_tensor_tensor(ls_pr[:, :], ls_gate[:, 0:8], 1.0, ls_gate[:, 12:20],
                                           ALU.add, ALU.mult).then_inc(ls_part, 1)
                    dve.wait_ge(ls_part, t * 6 + 3)
                    V.tensor_tensor(ls_2c[:, :], ls_pr[:, 0:4], ls_pr[:, 4:8], ALU.add).then_inc(ls_cell, 1)
                    dve.wait_ge(ls_cell, t * 2 + 2)
                    V.tensor_scalar(ls_gate[:, 16:20], ls_2c[:, :], 0.5, None, ALU.mult).then_inc(ls_cell, 1)
                    out_t = ls_out[:, :, bass.ds(t, 1)].rearrange("p c o -> p (c o)")
                    dve.wait_ge(ls_tanh, t + 1)
                    V.scalar_tensor_tensor(ls_parts[:, :, 0], ls_gate[:, 8:12], 1.0, ls_th[:, :],
                                           ALU.add, ALU.mult).then_inc(ls_h, 1)
                    V.scalar_tensor_tensor(ls_h2[:, :], ls_gate[:, 8:12], 1.0, ls_th[:, :],
                                           ALU.add, ALU.mult).then_inc(ls_part, 1)
                    dve.wait_ge(ls_h, t * 3 + 4)
                    dve.wait_ge(ls_part, t * 6 + 4)
                    V.tensor_tensor(ls_parts[:, :, 1], ls_h2[:, :], ls_parts[:, :, 0], ALU.subtract).then_inc(ls_h, 1)
                    V.tensor_tensor(ls_rest[:, :], ls_h2[:, :], ls_parts[:, :, 0], ALU.subtract).then_inc(ls_part, 1)
                    dve.wait_ge(ls_h, t * 3 + 5)
                    dve.wait_ge(ls_part, t * 6 + 5)
                    V.tensor_tensor(ls_parts[:, :, 2], ls_rest[:, :], ls_parts[:, :, 1], ALU.subtract).then_inc(ls_h, 1)
                    V.tensor_copy(out_t, ls_h2[:, :]).then_inc(ls_part, 1)

                dve.wait_ge(*evacd("L1f.gx3"))
                for u in range(2):
                    rank_hot(0, u)
                    step(u)
                    rank_place(0, u)
                with dve.Fori(1, ET // 2) as it:
                    for u in range(2):
                        dve.wait_ge(rk_seen, it * 2 + u)
                        rank_hot(it, u)
                        step(it * 2 + u)
                        rank_place(it, u)
                dve.wait_ge(rk_put, ET)
                dve.wait_ge(rk_seen, ET + 1)
                dve.wait_ge(attr_in, 16)
                make(V.tensor_scalar(place[0:EP, :], place_f[0:EP, :], 1.0, None, ALU.add), "sort.place")
                st.done(V.tensor_copy(table[0:EP, :, 0:2], ids[0:EP, :, :].rearrange("p j t -> p t j")))
                st.after()
                make(V.tensor_copy(table[0:EP, :, 2:10], attr[0:EP, :].rearrange("p (t c) -> p t c", c=8)), "sort.table")

                with dve.Fori(ET, N) as t:
                    step(t)
                dve.wait_ge(ls_part, 6 * N)
                for t in range(NT):
                    dve.wait_ge(*full("L1f.hs", t))
                    took(V.scalar_tensor_tensor(Xr[:, t, :], bank("L1f.hs", t)[0:R, :], 0.5, Xr[:, t, :],
                                                ALU.mult, ALU.add), "L1f.hs", t)
                dve.wait_ge(*evacd("L1f.hs"))

            if last >= 5:
                norm_x("L2")
                dve.wait_ge(*rows_ready(5))
                for b, x in ((2, "q"), (3, "k"), (4, "v")):
                    for t in range(NT):
                        dve.wait_ge(*full("L2.g" + x, t))
                        took(V.tensor_tensor(rowsof(B(b))[:, t, :], bank("L2.g" + x, t)[0:R, :], row("L2_gnn_b" + x),
                                             ALU.add), "L2.g" + x, t)
                dve.wait_ge(sorted_in, 32)
                make(V.tensor_copy(eidx[0:EP, :, :], sorted_e[0:EP, 1:ET + 1, 0:2].rearrange("p t j -> p j t")), "L2.idx")
                feature_maps("L2")
                attention("L2", ALU.add, 1e-6)
                add_out("L2.out", row("L2_mix_b_proj"), None)
                st.done(V.memset(zero5, 0.0))
                st.done(V.tensor_tensor(flag[0:EP, :], sorted_e[0:EP, 1:ET + 1, 0], sorted_e[0:EP, 0:ET, 0], ALU.is_equal))
                st.after()
                make(V.tensor_scalar(flag[0:EP, :], flag[0:EP, :], 1.0, BIG, ALU.subtract, ALU.mult), "L2.flag")
                with dve.Fori(0, ET // 4) as it:
                    for u in range(4):
                        dve.wait_ge(qk_in[u], it * 32 + 32)
                        V.tensor_tensor(prod, gat_q[u], gat_k[u], ALU.mult).then_inc(qk_used, 1)
                        dve.wait_ge(qk_used, it * 4 + (u + 1))
                        V.reduce_sum(logit[0:EP, bass.ds(it * 4 + u, 1), :].rearrange("p o h -> p (o h)"),
                                     prod.rearrange("p (h d) -> p h d", h=H), AX_X).then_inc(qk_prod, 1)
                        dve.wait_ge(qk_prod, it * 4 + (u + 1))
                make(V.scalar_tensor_tensor(logit[0:EP, :, :], logit[0:EP, :, :], 0.125, sorted_e[0:EP, 1:ET + 1, 2:10],
                                            ALU.mult, ALU.add), "L2.logit")
                st.done(V.memset(frow[:, E:E + 1], 0.0))
                dve.wait_ge(qkv_out, 48)
                for j in range(20):
                    dve.wait_ge(*full("L2.fT", j))
                    took(V.tensor_copy(frow[:, 0:E].rearrange("h (p t) -> h t p", t=ET)[:, 4 * j:4 * j + 4, :],
                                       bank("L2.fT", j)[0:8, 0:500].rearrange("h (q p) -> h q p", q=4)), "L2.fT", j)
                dve.wait_ge(*evacd("L2.fT"))
                dve.wait_ge(*evacd("L2.lT"))
                st.after()
                st.done(V.tensor_tensor_scan(lrow, frow[:, 0:E], lrow, -BIG, ALU.add, ALU.max))
                st.after()
                make(V.tensor_tensor_scan(lrow[:, ::-1], frow[:, 1:E + 1][:, ::-1], lrow[:, ::-1], -BIG, ALU.add, ALU.max),
                     "L2.rowmax")
                for j in range(2):
                    dve.wait_ge(*full("L2.mR", j))
                    took(V.tensor_tensor(logit[0:EP, 40 * j:40 * j + 40, :], logit[0:EP, 40 * j:40 * j + 40, :],
                                         bank("L2.mR", j)[0:EP, 0:320].rearrange("p (t h) -> p t h", h=H),
                                         ALU.subtract), "L2.mR", j)
                dve.wait_ge(*made("L2.pexp"))

                def weigh(it, u):
                    p = logit[0:EP, bass.ds(it * 2 + u, 1), :].rearrange("p o h -> p (o h)")
                    V.tensor_scalar(hot_s[u], iota[0:EP, :], sorted_e[0:EP, bass.ds(it * 2 + (u + 1), 1), 0], None,
                                    ALU.is_equal).then_inc(pv_ready, 1)
                    V.tensor_copy(pv[u][:, 512:520], p).then_inc(pv_ready, 1)
                    dve.wait_ge(v_in[u], it * 16 + 16)
                    V.tensor_tensor(pv[u][:, 0:512].rearrange("p (h d) -> p h d", h=H),
                                    gat_v[u].rearrange("p (h d) -> p h d", h=H),
                                    p.unsqueeze(2).to_broadcast([EP, H, 64]), ALU.mult).then_inc(pv_ready, 1)
                    dve.wait_ge(pv_ready, it * 6 + (3 * u + 3))
                    V.memset(small[0:1, 40 + u:41 + u], 0.0).then_inc(v_used, 1)
                for u in range(2):
                    weigh(0, u)
                with dve.Fori(1, ET // 2) as it:
                    for u in range(2):
                        dve.wait_ge(pv_used, it * 2 + (u - 1))
                        weigh(it, u)
                dve.wait_ge(pv_used, ET)
                st.done(V.tensor_scalar(den[0:R, :, :], PSF[0:R, 2560:2600].rearrange("p (t h) -> p t h", t=NT),
                                        1e-30, None, ALU.max))
                st.after()
                st.done(V.reciprocal(den[0:R, :, :], den[0:R, :, :]))
                st.after()
                for t in range(NT):
                    make(V.tensor_tensor(rowsof(B(3))[:, t, :].rearrange("p (h d) -> p h d", h=H),
                                         PSF[0:R, 512 * t:512 * t + 512].rearrange("p (h d) -> p h d", h=H),
                                         den[0:R, t, :].unsqueeze(2).to_broadcast([R, H, 64]), ALU.mult), "L2.ysum")
                add_out("L2.gout", row("L2_gnn_bo"), "L2.done")

            if last >= 6:
                norm_x("L2f")
                dve.wait_ge(*rows_ready(6))
                softmax_small("L2f", "L2f.lg", 8)
                p = sm[0:R, 7, :, :]
                over_sum(None, p, sm[0:R, 1, :, :], 8)
                st.after()
                hot2 = pick2(p, 8)
                st.done(V.tensor_tensor(p, p, hot2, ALU.mult))
                st.after()
                comb = sm[0:R, 0, :, :]
                over_sum("L2f", comb, p, 8, tiny=1e-20)
                dve.wait_ge(*made("L2f.prob"))
                add_out("L2f.s2", row("L2_ffn_sb2"), None)
                for j in range(2):
                    stage = f"L2f.eo{j}"
                    for e in range(4):
                        for t in range(NT):
                            i = 5 * e + t
                            dve.wait_ge(*full(stage, i))
                            if i >= 5:
                                dve.wait_ge(*evacd(stage, i - 5))
                            elif j:
                                dve.wait_ge(*evacd("L2f.eo0", 15 + t))
                            took(V.scalar_tensor_tensor(Xr[:, t, :], bank(stage, i)[0:R, :],
                                                        comb[:, t, 4 * j + e:4 * j + e + 1], Xr[:, t, :],
                                                        ALU.mult, ALU.add), stage, i)
                dve.wait_ge(*evacd("L2f.eo1"))

            if last >= 7:
                norm_x("L3")
                dve.wait_ge(*rows_ready(7))
                for t in range(NT):
                    make(V.tensor_tensor(AC[0:R, t, t * R:(t + 1) * R], AC[0:R, t, t * R:(t + 1) * R], ident[0:R, 0:R],
                                         ALU.add), "L3.selfs")
                make(V.memset(xp[:, :, :, 128:129], 1.0), "L3.onec")
                att = rowsof(B(6))
                dve.wait_ge(*evacd("L3.xp"))
                for j, x in enumerate(("L3_gnn_att_src", "L3_gnn_att_dst")):
                    for t in range(NT):
                        st.done(V.tensor_tensor(att[:, t, 256 * j:256 * j + 256].rearrange("p (h f) -> p h f", h=2),
                                                xp[:, t, :, 0:128],
                                                row(x, 256).rearrange("p (h f) -> p h f", h=2), ALU.mult))
                st.after()
                for j in range(2):
                    for t in range(NT):
                        make(V.reduce_sum(sd[0:R, 2 * j:2 * j + 2, t],
                                          att[:, t, 256 * j:256 * j + 256].rearrange("p (h f) -> p h f", h=2), AX_X),
                             "L3.sd")
                for t in range(NT):
                    dve.wait_ge(*full("L3.adjT", t))
                    took(V.tensor_scalar(AH[0:R, t, :].rearrange("p (s n) -> p s n", s=NT),
                                         slot("L3.adjT", t)[0:R, 0:640].rearrange("p (s n) -> p s n", s=NT)[:, :, 0:R],
                                         0.0, -BIG, ALU.is_equal, ALU.mult), "L3.adjT", t)
                dve.wait_ge(*evacd("L3.adjT"))
                dve.wait_ge(*evacd("L3.sdB"))
                dve.wait_ge(*made("L3.sd"))
                for h in range(2):
                    for t in range(NT):
                        st.done(V.tensor_tensor_reduce(out=pT[:, 5 * h + t, :],
                                                       in0=AH[0:R, t, :], in1=sB[:, h, :], scale=1.0, scalar=-3.0e38,
                                                       op0=ALU.add, op1=ALU.max, accum_out=mxc[0:R, h, t:t + 1]))
                st.after()
                st.done(V.tensor_tensor(mxc[0:R, :, :], mxc[0:R, :, :], sd[0:R, 2:4, :], ALU.add))
                st.after()
                make(V.scalar_tensor_tensor(mxc[0:R, :, :], mxc[0:R, :, :], 0.2, mxc[0:R, :, :], ALU.mult, ALU.max), "L3.mx")
                for h in range(2):
                    for s in range(NT):
                        j = 5 * h + s
                        st.done(V.tensor_scalar(pT[:, j, :], sB[:, 2 + h, :], sd[0:R, h, s:s + 1], None, ALU.add))
                st.after()
                for j in range(10):
                    st.done(V.scalar_tensor_tensor(pT[:, j, :], pT[:, j, :], 0.2, pT[:, j, :], ALU.mult, ALU.max))
                st.after()
                dve.wait_ge(*evacd("L3.mxB"))
                for j in range(10):
                    make(V.tensor_tensor(pT[:, j, :], pT[:, j, :], mB[:, j // 5, :], ALU.subtract), "L3.sub")
                for j in range(10):
                    dve.wait_ge(*made("L3.pexp", j + 1))
                    make(V.tensor_tensor(pT[:, j, :], pT[:, j, :], AC[0:R, j % 5, :], ALU.mult), "L3.pt")
                for t in range(NT):
                    dve.wait_ge(*full("L3.gat", t))
                    o = bank("L3.gat", t)[0:R, 0:258].rearrange("p (h f) -> p h f", h=2)
                    st.done(V.tensor_scalar(den[0:R, t, 0:2], o[:, :, 128], 1e-16, None, ALU.max))
                    st.after()
                    st.done(V.reciprocal(den[0:R, t, 0:2], den[0:R, t, 0:2]))
                    st.after()
                    og3 = og[:, t, :].rearrange("p (h f) -> p h f", h=2)
                    took(V.tensor_tensor(og3, o[:, :, 0:128], den[0:R, t, 0:2].unsqueeze(2).to_broadcast([R, 2, 128]),
                                         ALU.mult), "L3.gat", t)
                    dve.wait_ge(*evacd("L3.gat", t))
                    make(V.tensor_tensor(og[:, t, :], og[:, t, :], row("L3_gnn_bias_g", 256), ALU.add), "L3.og")
                add_out("L3.gout", row("L3_gnn_b3"), None)
                for stage, dst, bias in (("L3.k", kR, "L3_mix_bk"), ("L3.v", vR, "L3_mix_bv")):
                    for t in range(NT):
                        dve.wait_ge(*full(stage, t))
                        took(V.tensor_tensor(dst[:, t, :], bank(stage, t)[0:R, :], row(bias), ALU.add), stage, t)
                feature_maps("L3")
                attention("L3", ALU.max, 1e-6)
                for t in range(NT):
                    dve.wait_ge(*full("L3.out", t))
                    took(V.tensor_tensor(u5[:, t, :], bank("L3.out", t)[0:R, :], row("L3_mix_bo"), ALU.add), "L3.out", t)
                    dve.wait_ge(*evacd("L3.out", t))
                    st.done(V.tensor_tensor(u5[:, t, :], u5[:, t, :], xn[:, t, :], ALU.add))
                st.after()

                def put3(t, m, r):
                    st.done(V.tensor_scalar(u5[:, t, :], u5[:, t, :], m, r, ALU.subtract, ALU.mult))
                normalize(u5, put3)
                st.after()
                for t in range(NT):
                    st.done(V.tensor_tensor(u5[:, t, :], u5[:, t, :], row("L3_mix_gamma"), ALU.mult))
                st.after()
                for t in range(NT):
                    st.done(V.tensor_tensor(Xr[:, t, :], Xr[:, t, :], row("L3_mix_beta"), ALU.add))
                st.after()
                for t in range(NT):
                    make(V.tensor_tensor(Xr[:, t, :], Xr[:, t, :], u5[:, t, :], ALU.add), "L3.done")
                dve.wait_ge(*made("L3.done"))

            if last >= 8:
                norm_x("L3f")
                dve.wait_ge(*rows_ready(8))
                lg = softmax_small("L3f", "L3f.lg", 8, bias=row("L3_ffn_router_b", 8).unsqueeze(1).to_broadcast([R, NT, 8]))
                hot2 = pick2(lg, 8)
                p = sm[0:R, 7, :, :]
                st.done(V.tensor_tensor(p, sm[0:R, 1, :, :], hot2, ALU.mult))
                st.after()
                comb = sm[0:R, 0, :, :]
                over_sum("L3f", comb, p, 8)
                dve.wait_ge(*made("L3f.prob"))
                for t in range(NT):
                    dve.wait_ge(*full("L3f.b", t))
                    took(V.tensor_tensor(Xr[:, t, :], bank("L3f.b", t)[0:R, :], Xr[:, t, :], ALU.add), "L3f.b", t)

                def add_expert(e):
                    before = "L3f.b" if e == 0 else f"L3f.y{e - 1}"
                    for t in range(NT):
                        dve.wait_ge(*full(f"L3f.y{e}", t))
                        dve.wait_ge(*evacd(before, t))
                        took(V.scalar_tensor_tensor(Xr[:, t, :], bank(f"L3f.y{e}", t)[0:R, :], comb[:, t, e:e + 1],
                                                    Xr[:, t, :], ALU.mult, ALU.add), f"L3f.y{e}", t)
                for e in range(8):
                    gi, gg, go, hh = colsof(B(2)), colsof(B(3)), colsof(B(4)), colsof(B(5 + e % 2))
                    dve.wait_ge(*evacd(f"L3f.i{e}"))
                    dve.wait_ge(*evacd(f"L3f.g{e}"))
                    make(V.tensor_tensor(gi, gi, gg, ALU.mult), f"L3f.cell{e}")
                    if e:
                        add_expert(e - 1)
                    dve.wait_ge(*evacd(f"L3f.o{e}"))
                    dve.wait_ge(*made(f"L3f.tc{e}"))
                    make(V.tensor_tensor(hh, go, gi, ALU.mult), f"L3f.hid{e}")
                add_expert(7)

        for name, k in [m[:2] for m in MADE if m[2] <= last] + [t[:2] for t in tiles]:
            assert emitted.get(name, 0) == k, name


def kernel(**inputs):
    import numpy as np
    import concourse.bacc as bacc
    from concourse.bass_utils import run_bass_kernel_spmd as run

    a = {k: np.asarray(v) for k, v in inputs.items()}

    def chunked(w):
        k = w.shape[0] // 128
        return np.ascontiguousarray(w.reshape(k, 128, w.shape[1]).transpose(1, 0, 2))

    w = {}
    for i in range(3):
        w[f"L0_gnn_Wl{i}"] = a[f"L0_gnn_Wl{i}"].T
        w[f"L0_gnn_Wr{i}"] = a[f"L0_gnn_Wr{i}"].T
    for j, x in enumerate(("q", "k", "v")):
        w["L0_w" + x] = a["L0_mix_w_qkv"][j * 512:(j + 1) * 512].T
        w["L2_w" + x] = a["L2_mix_w_qkv"][:, j * 512:(j + 1) * 512]
        w["L3_w" + x] = a["L3_mix_W" + x]
    w["L0_wo"] = a["L0_mix_w_out"].T
    w["L2_wo"] = a["L2_mix_w_proj"]
    w["L3_wo"] = a["L3_mix_Wo"]
    for lv in range(2):
        w[f"L0_ffn_W1_{lv}"] = a[f"L0_ffn_W1_{lv}"].transpose(1, 0, 2).reshape(512, -1)
        w[f"L0_ffn_W2_{lv}"] = a[f"L0_ffn_W2_{lv}"].reshape(-1, 512)
    for name in ("L1_gnn_W_self1", "L1_gnn_W_neigh1", "L1_gnn_W_self2", "L1_gnn_W_neigh2", "L1_mix_W_in", "L1_mix_W_out",
                 "L2_gnn_Wq", "L2_gnn_Wk", "L2_gnn_Wv", "L2_gnn_Wo", "L2_ffn_sw1", "L2_ffn_sw2",
                 "L3_gnn_W1", "L3_gnn_W2", "L3_gnn_Wg", "L3_gnn_W3"):
        w[name] = a[name]
    for x in "fioc":
        w["L1_wx_" + x] = a["L1_ffn_W_" + x][:512]
        w["L1_wh_" + x] = a["L1_ffn_W_" + x][512:]
    for j in range(2):
        w[f"L2_w1_{j}"] = a["L2_ffn_w1"][4 * j:4 * j + 4].transpose(1, 0, 2).reshape(512, 512)
        w[f"L2_w2_{j}"] = a["L2_ffn_w2"][4 * j:4 * j + 4].reshape(512, 512)
    for e in range(8):
        w[f"L3_wi{e}"] = a["L3_ffn_Wi"][e, :, 0:512]
        w[f"L3_wg{e}"] = a["L3_ffn_Wi"][e, :, 1024:1536]
        w[f"L3_wo_{e}"] = a["L3_ffn_Wi"][e, :, 1536:2048]
        w[f"L3_wout{e}"] = a["L3_ffn_Wo"][e]

    halves = {t[0]: t[3] for t in TILES}
    used = [x[0] for x in WEIGHTS if (4 if x[3].startswith("split") else halves[x[3]]) <= LAST]
    arrays = {name: chunked(w[name]) for name in used}
    arrays["x"] = a["x"]
    arrays["edges"] = np.ascontiguousarray(
        np.stack([a["src"].reshape(ET, EP).T, a["dst"].reshape(ET, EP).T], axis=1))
    table = np.zeros((len(ROWS), NROWS * D), np.float32)
    for n, half in enumerate(ROW_HALVES):
        for j, name in enumerate(ROWS[half]):
            v = a[name].reshape(-1)
            table[n, j * D:j * D + v.size] = v
    arrays["rows"] = table
    col = []
    for name, k in COLS:
        if name == "a_prelu":
            col.append(np.broadcast_to(a["L0_gnn_a_prelu"].reshape(1, 1), (128, 1)))
        else:
            col.append(a[name].reshape(k, 128).T)
    arrays["cols"] = np.ascontiguousarray(np.concatenate(col, axis=1))
    routers = np.zeros((128, 4, 4, 8), np.float32)
    for j, m in enumerate((a["L0_ffn_Wr0"], a["L0_ffn_Wr1"], a["L2_ffn_gate_w"].T, a["L3_ffn_router_w"])):
        routers[:, j, :, 0:m.shape[1]] = chunked(m)
    arrays["routers"] = routers
    eb = np.zeros((len(EBIAS), 8, 2, 512), np.float32)
    for n, half in enumerate(sorted(EBIAS)):
        for j, name in enumerate(EBIAS[half]):
            eb[n, 0:a[name].shape[0], j] = a[name]
    arrays["ebias"] = eb
    for name in ("L1_mix_Wq", "L1_mix_Wk", "L1_mix_Wv"):
        arrays[name] = a[name]
    arrays["attr"] = np.ascontiguousarray(a["edge_attr_8"].reshape(ET, EP, 8).transpose(1, 0, 2)).reshape(EP, ET * 8)

    nc = bacc.Bacc("TRN2", target_bir_lowering=False, num_devices=1)
    io, fed = {}, {}
    for name, v in arrays.items():
        v = np.ascontiguousarray(v)
        fed["in_" + name] = v
        io[name] = nc.dram_tensor("in_" + name, v.shape, mybir.dt.from_np(v.dtype), kind="ExternalInput").ap()
    io["out"] = nc.dram_tensor("result", (N, D), F32, kind="ExternalOutput").ap()
    network(nc, io, LAST)
    r = run(nc, [fed], core_ids=[0])
    return r.results[0]["result"]
```
